# Optimizing a Trainium2 kernel written in Bass

```python
import numpy as np
import jax
import jax.numpy as jnp

def _softmax(x, axis=-1):
    return jax.nn.softmax(x, axis=axis)

def _gelu(x):
    return jax.nn.gelu(x, approximate=True)

def _silu(x):
    return jax.nn.silu(x)

def _sigmoid(x):
    return jax.nn.sigmoid(x)

def _layernorm(x, axis=-1, eps=1e-05):
    m = jnp.mean(x, axis=axis, keepdims=True)
    v = jnp.var(x, axis=axis, keepdims=True)
    return (x - m) / jnp.sqrt(v + eps)

def _scatter_add(tgt, idx, src, axis=0):
    return tgt.at[idx].add(src)

def _segment_sum(src, seg, n):
    return jax.ops.segment_sum(src, seg, n)
kernel_name = 'mk_prb_d1_jaxref_r4_b1caac'

def setup_inputs(seed: int=0):
    np.random.seed(seed)
    _w = jnp.asarray

    def _L0_attn_setup():
        import jax, jax.numpy as jnp
        import numpy as np
        H = 16
        G = 16
        R = 4
        WIN = 64
        NEG = -1000000000.0
        key = jax.random.key(seed)
        ks = jax.random.split(key, 9)
        dm, D = (256, 256 // H)
        s = 0.02
        return {'x': jax.random.normal(ks[0], (1, 512, dm), dtype=jnp.float32), 'Wq': jax.random.normal(ks[1], (dm, dm), dtype=jnp.float32) * s, 'Wk': jax.random.normal(ks[2], (dm, dm), dtype=jnp.float32) * s, 'Wv': jax.random.normal(ks[3], (dm, dm), dtype=jnp.float32) * s, 'Wo': jax.random.normal(ks[4], (dm, dm), dtype=jnp.float32) * s, 'Wck': jax.random.normal(ks[5], (G * D, D), dtype=jnp.float32) * s, 'Wcv': jax.random.normal(ks[6], (G * D, D), dtype=jnp.float32) * s, 'Wg': jax.random.normal(ks[7], (D, 3), dtype=jnp.float32) * s, 'bg': jnp.zeros((3,), dtype=jnp.float32)}
    _L0_attn_in = _L0_attn_setup()

    def _L0_ffn_setup():
        import jax, jax.numpy as jnp
        import numpy as np
        E = 8
        K = 2
        CAP_FACTOR = 1.0
        key = jax.random.key(seed)
        k0, k1, k2, k3 = jax.random.split(key, 4)
        B, S, M, H = (4, 512, 256, 1024)
        x = jax.random.normal(k0, (B, S, M), jnp.float32)
        wg = jax.random.normal(k1, (M, E), jnp.float32) * 0.02
        w1 = jax.random.normal(k2, (E, M, H), jnp.float32) * 0.02
        b1 = jnp.zeros((E, H), jnp.float32)
        w2 = jax.random.normal(k3, (E, H, M), jnp.float32) * 0.02
        b2 = jnp.zeros((E, M), jnp.float32)
        return {'x': x, 'wg': wg, 'w1': w1, 'b1': b1, 'w2': w2, 'b2': b2}
    _L0_ffn_in = _L0_ffn_setup()
    _d = {'L0_attn_x': _L0_attn_in['x'], 'L0_attn_Wq': _L0_attn_in['Wq'], 'L0_attn_Wk': _L0_attn_in['Wk'], 'L0_attn_Wv': _L0_attn_in['Wv'], 'L0_attn_Wo': _L0_attn_in['Wo'], 'L0_attn_Wck': _L0_attn_in['Wck'], 'L0_attn_Wcv': _L0_attn_in['Wcv'], 'L0_attn_Wg': _L0_attn_in['Wg'], 'L0_attn_bg': _L0_attn_in['bg'], 'L0_ffn_wg': _L0_ffn_in['wg'], 'L0_ffn_w1': _L0_ffn_in['w1'], 'L0_ffn_b1': _L0_ffn_in['b1'], 'L0_ffn_w2': _L0_ffn_in['w2'], 'L0_ffn_b2': _L0_ffn_in['b2']}
    _x0 = _d['L0_attn_x']
    _d['L0_attn_x'] = jax.random.normal(jax.random.fold_in(jax.random.key(seed), 1), (4, 2048, 256), dtype=_x0.dtype)
    del _x0
    return _d

def reference(L0_attn_x, L0_attn_Wq, L0_attn_Wk, L0_attn_Wv, L0_attn_Wo, L0_attn_Wck, L0_attn_Wcv, L0_attn_Wg, L0_attn_bg, L0_ffn_wg, L0_ffn_w1, L0_ffn_b1, L0_ffn_w2, L0_ffn_b2):

    def _L0_attn_ref(x, Wq, Wk, Wv, Wo, Wck, Wcv, Wg, bg):
        import jax, jax.numpy as jnp
        import numpy as np
        H = 16
        G = 16
        R = 4
        WIN = 64
        NEG = -1000000000.0
        B, T, dm = x.shape
        D = dm // H
        scale = float(np.sqrt(D))

        def split_heads(y):
            return y.reshape(B, T, H, D).transpose(0, 2, 1, 3)
        q = split_heads(x @ Wq)
        k = split_heads(x @ Wk)
        v = split_heads(x @ Wv)
        pad = -T % G
        T_pad = T + pad
        k_pad = jnp.pad(k, ((0, 0), (0, 0), (0, pad), (0, 0)))
        v_pad = jnp.pad(v, ((0, 0), (0, 0), (0, pad), (0, 0)))
        nb = T_pad // G
        k_c = k_pad.reshape(B, H, nb, G * D) @ Wck
        v_c = v_pad.reshape(B, H, nb, G * D) @ Wcv
        pos = jnp.arange(T)
        blk_end = (jnp.arange(nb) + 1) * G
        c_ok = pos[:, None] >= blk_end[None, :]
        s_b = jnp.einsum('bhtd,bhnd->bhtn', q, k_c) / scale
        logits_c = jnp.where(c_ok, s_b, NEG)
        out_c = jnp.einsum('bhtn,bhnd->bhtd', jax.nn.softmax(logits_c, axis=-1), v_c)
        out_c = out_c * jnp.any(c_ok, axis=-1)[:, None].astype(out_c.dtype)
        r_eff = min(R, nb)
        _, top_idx = jax.lax.top_k(logits_c, r_eff)
        tok = (top_idx[..., None] * G + jnp.arange(G)).reshape(B, H, T, r_eff * G)
        tok = jnp.clip(tok, 0, T_pad - 1)
        bi = jnp.arange(B)[:, None, None, None]
        hi = jnp.arange(H)[None, :, None, None]
        k_s = k_pad[bi, hi, tok]
        v_s = v_pad[bi, hi, tok]
        allowed = tok <= pos[None, None, :, None]
        logits_s = jnp.where(allowed, jnp.einsum('bhtd,bhtnd->bhtn', q, k_s) / scale, NEG)
        out_s = jnp.einsum('bhtn,bhtnd->bhtd', jax.nn.softmax(logits_s, axis=-1), v_s)
        out_s = out_s * jnp.any(allowed, axis=-1)[..., None].astype(out_s.dtype)
        wmask = (jnp.abs(pos[:, None] - pos[None, :]) <= WIN // 2) & (pos[:, None] >= pos[None, :])
        logits_l = jnp.where(wmask, jnp.einsum('bhtd,bhsd->bhts', q, k) / scale, NEG)
        out_l = jnp.einsum('bhts,bhsd->bhtd', jax.nn.softmax(logits_l, axis=-1), v)
        gates = jax.nn.softmax(q.mean(axis=1) @ Wg + bg, axis=-1)

        def merge(o):
            return o.transpose(0, 2, 1, 3).reshape(B, T, dm)
        out = gates[..., 0:1] * merge(out_c) + gates[..., 1:2] * merge(out_s) + gates[..., 2:3] * merge(out_l)
        return out @ Wo

    def _L0_ffn_ref(x, wg, w1, b1, w2, b2):
        import jax, jax.numpy as jnp
        import numpy as np
        E = 8
        K = 2
        CAP_FACTOR = 1.0
        B, S, M = x.shape
        N = B * S
        capacity = int(CAP_FACTOR * K * N // E)
        xt = x.reshape(N, M)
        logits = xt @ wg
        scores = jax.nn.softmax(logits, axis=-1)
        topv, topi = jax.lax.top_k(scores, K)
        topv = topv / jnp.sum(topv, axis=-1, keepdims=True)
        masks = jax.nn.one_hot(topi.T, E, dtype=jnp.int32)
        flat = masks.reshape(K * N, E)
        locs = jnp.cumsum(flat, axis=0) - 1
        pos = jnp.sum(locs * flat, axis=-1).reshape(K, N).T
        valid = pos < capacity
        gate = topv * valid.astype(topv.dtype)
        pos_c = jnp.where(valid, pos, 0)
        xk = xt[:, None, :] * valid[..., None].astype(xt.dtype)
        disp = jnp.zeros((E, capacity, M), xt.dtype)
        disp = disp.at[topi, pos_c].add(xk)
        h = jax.nn.relu(jnp.einsum('ecm,emh->ech', disp, w1) + b1[:, None, :])
        y = jnp.einsum('ech,ehm->ecm', h, w2) + b2[:, None, :]
        out = jnp.sum(gate[..., None] * y[topi, pos_c], axis=1)
        return out.reshape(B, S, M)
    x = L0_attn_x
    xn = _layernorm(x, axis=-1)
    x = x + _L0_attn_ref(xn, L0_attn_Wq, L0_attn_Wk, L0_attn_Wv, L0_attn_Wo, L0_attn_Wck, L0_attn_Wcv, L0_attn_Wg, L0_attn_bg) + _L0_ffn_ref(xn, L0_ffn_wg, L0_ffn_w1, L0_ffn_b1, L0_ffn_w2, L0_ffn_b2)
    return x

_drawn_inputs = setup_inputs


def setup_inputs(seed=0):
    import zlib

    import numpy as np

    out = dict(_drawn_inputs(seed))
    spreads = {'L0_attn_bg': (0.0, 0.8), 'L0_ffn_b1': (0.0, 0.8), 'L0_ffn_b2': (0.0, 0.53)}
    factors = {'L0_attn_Wq': 8.0,
     'L0_attn_Wk': 8.0,
     'L0_attn_Wv': 6.656,
     'L0_attn_Wo': 6.631,
     'L0_attn_Wck': 8.0,
     'L0_attn_Wcv': 8.0,
     'L0_attn_Wg': 8.0,
     'L0_ffn_w1': 3.087}
    for name, (base, spread) in spreads.items():
        noise = np.random.default_rng([zlib.crc32(name.encode()), seed]).standard_normal(out[name].shape)
        drawn = base * np.exp(spread * noise) if base else spread * noise
        out[name] = jnp.asarray(drawn.astype(out[name].dtype))
    for name, factor in factors.items():
        out[name] = (out[name] * factor).astype(out[name].dtype)
    return out
```

```python
from contextlib import ExitStack

import concourse.bass as bass
from concourse import mybir

F32 = mybir.dt.float32
BF16 = mybir.dt.bfloat16
I32 = mybir.dt.int32
U32 = mybir.dt.uint32
ALU = mybir.AluOpType
ACT = mybir.ActivationFunctionType
AX = mybir.AxisListType

P = 128
B, T, DM = 4, 2048, 256
H, D = 16, 16
G = 16
NB = T // G
NT = T // P
CH = 512
NC = T // CH
BH = B * H
TK = T + NB
QK = 6 * D
NM = 9
ROWS = QK + NM
WIN = 32
LW = P + WIN
E, KTOP, HID = 8, 2, 1024
N = B * T
CAP = KTOP * N // E
NEG = -(2.0 ** 30)
FAR = -3.0e38
FOUND = 3.0e38
EPS = 1e-5
TP = NT + 1


def banks_of(c):
    t = 4 * c
    window = [("L", t - 1, 0, WIN, 0)] if c else []
    window += [("L", t + r, P * r, LW, WIN + LW * r) for r in range(3)]
    return ([[("C", NT, 0, CH, 0)], window, [("S", t, 0, CH, 0)],
             [("S", t + 1, P, 3 * P, 0), ("S", t + 3, 3 * P, P, 3 * P)]]
            + [[("S", j, 0, CH, 0)] for j in range(t)]
            + [[("S", t + 2, 2 * P, 2 * P, 0), ("L", t + 3, 3 * P, P, 2 * P)]])


def ahead_of(c):
    return ([("scs", 0, 0), ("loc", 0, 0), ("loc", 1, 0)]
            + [("S", r, kk) for r in range(4) for kk in range(c + 1)])


SEQ = list(range(NC)) + list(range(NC))[::-1]


def chunk_of(ls):
    return SEQ[ls % (2 * NC)]


def units_of(c):
    return 4 * c + 5


def ring_cost(kind, kk, c):
    if kind == "S":
        return 560 if kk < c else 380
    return {"scs": 500, "loc": 420}[kind]


def step_plan(c, nxt, first=False):
    base = []
    for u in range(units_of(c)):
        base.append(("scores", u))
        if u % 4 == 1 and u > 4:
            base.append(("values", u // 4 - 1))
    if c == 0 or (units_of(c) - 1) % 4 < 1:
        base.append(("values", c))
    ahead = ahead_of(nxt) if nxt is not None else []
    cost = {"scores": 430, "values": 900}
    room = sum(cost[b[0]] for b in base) - TAIL
    need, t = [], START
    for n_, (kind, r, kk) in enumerate(ahead):
        t += ring_cost(kind, kk, nxt) + (CHOOSE if n_ + 1 in (AT_TOP, AT_FOUND) else 0)
        need.append(t)
    total = need[-1] if need else 1
    scale = min(1.0, room / total)
    order, pe, done = [], 0, 0
    for item in base:
        while done < len(ahead) and (need[done - RING] * scale if done >= RING else done * FIRST) <= pe:
            order.append(("ring",) + ahead[done])
            done += 1
        order.append(item)
        pe += cost[item[0]]
    tail = order.pop()
    order += [("ring",) + a for a in ahead[done:]]
    if nxt is not None:
        order += [("ring", "maskT", 0, 0), tail, ("maxrows",)]
    else:
        order.append(tail)
    if not first:
        order.append(("ring", "out", 0, 0))
    order.append(("values", c + 1))
    return order


START, CHOOSE, TAIL, FIRST = -300, 400, 2000, 0


AT_TOP, AT_FOUND = 3, 5
RING = 3
SLOTS = 3
CONSUMER = {"scs": "A", "loc": "D", "S": "D", "maskT": "A", "out": "D"}


class Ring:

    def __init__(self):
        self.unit, self.freed, self.owners = 0, {"A": 0, "D": 0}, []

    def next(self, kind):
        before = self.owners[-RING] if len(self.owners) >= RING else None
        u = self.unit
        self.unit += 1
        self.freed[CONSUMER[kind]] += 1
        self.owners.append((CONSUMER[kind], self.freed[CONSUMER[kind]]))
        return u, before

    def through(self, steps):
        for ls in steps:
            for it in step_plan(chunk_of(ls), chunk_of(ls + 1), ls == 0):
                if it[0] == "ring":
                    self.next(it[1])
        return self


PRO = ahead_of(0) + [("maskT", 0, 0)]


def ring_at_body():
    r = Ring()
    for kind, _, _ in PRO:
        r.next(kind)
    r.through([0])
    r.owners = [("D", r.freed["D"] - 1), ("A", r.freed["A"]), ("D", r.freed["D"])]
    return r


def ring_per_body():
    a, b = ring_at_body(), ring_at_body().through(range(1, 2 * NC + 1))
    return b.unit - a.unit, b.freed["A"] - a.freed["A"], b.freed["D"] - a.freed["D"]


RU, RA, RD = ring_per_body()
assert RU % RING == 0
UNITS_H = sum(units_of(c) for c in range(NC))
GROUPS_H = sum(c + 2 for c in range(NC))


def unit_before(ls):
    return sum(units_of(chunk_of(x)) for x in range(ls))


def slot_of(ls, u):
    v = unit_before(ls if ls else 2 * NC) - units_of(0) + u
    return v % SLOTS, v == 0 and (2 * UNITS_H - 1) % SLOTS == 0


def group_before(ls):
    return sum(chunk_of(x) + 2 for x in range(ls))


def land(eng, sem):
    eng.sem_inc(sem, 1)


def phase_a(nc, d, big):
    with ExitStack() as ctx:
        def sb(name, shape, dt=F32):
            return ctx.enter_context(nc.sbuf_tensor(name, shape, dt))

        def sem(name):
            return ctx.enter_context(nc.semaphore(name))

        bank = [ctx.enter_context(nc.psum_tensor(f"a_bank{i}", [P, CH], F32)) for i in range(8)]
        ident = sb("a_ident", [P, P])
        W = {n: sb(f"a_w{n}", [P, 2, DM]) for n in "qkv"}
        WCK = sb("a_wck", [P, G, P])
        WCV = sb("a_wcv", [P, G, P])
        WG = sb("a_wgate", [P, 3])
        WR = sb("a_wrouter", [P, 2, E])
        eps = sb("a_eps", [P, 1])
        xin = [sb(f"a_xin{i}", [P, 4, DM]) for i in range(2)]
        xn = [sb(f"a_xn{i}", [P, 4, DM]) for i in range(2)]
        xnT = [sb(f"a_xnT{i}", [P, 2, CH]) for i in range(2)]
        st = sb("a_st", [P, 4, 6])
        mv = sb("a_mv", [P, 4, 2])
        std = sb("a_std", [P, 4])
        rstd = sb("a_rstd", [P, 4])
        qT = sb("a_qT", [P, 2, CH])
        kT = sb("a_kT", [P, 2, T])
        vT = sb("a_vT", [P, 2, T])
        part = {n: [sb(f"a_{n}part{i}", [P, 3, 2, CH], BF16) for i in range(2)] for n in "qk"}
        rest = {n: sb(f"a_{n}rest", [P, 2, CH]) for n in "qk"}
        cpart = sb("a_cpart", [P, 3, 2, NB], BF16)
        crest = sb("a_crest", [P, 2, NB])
        vcT = sb("a_vcT", [P, 2, NB])

        const_in = sem("a_const_in")
        zeroed = sem("a_zeroed")
        x_in = [sem(f"a_x_in{i}") for i in range(2)]
        xn_out = [sem(f"a_xn_out{i}") for i in range(2)]
        part_out = [sem(f"a_part_out{i}") for i in range(2)]
        cpart_out = sem("a_cpart_out")
        stats1 = sem("a_stats1")
        stats = sem("a_stats")
        std_ok = sem("a_std_ok")
        rstd_ok = sem("a_rstd_ok")
        xn_ok = sem("a_xn_ok")
        ring_full = sem("a_ring_full")
        freed = {"A": sem("a_freed_act"), "D": sem("a_freed_dve")}
        proj = sem("a_proj")
        first_ok = sem("a_first_ok")
        rest_ok = sem("a_rest_ok")
        vT_ok = sem("a_vT_ok")
        second_ok = sem("a_second_ok")
        third_ok = sem("a_third_ok")
        c1_ok = sem("a_c1_ok")
        vcT_ok = sem("a_vcT_ok")

        per_chunk = [("xT0", "A"), ("xT1", "D"), ("gr", "D"), ("vt0", "A"), ("vt1", "D")]
        seq = per_chunk * 4 + [("kcvc", "D"), ("vcT", "D")]
        UB, AB, DB = len(seq), sum(s[1] == "A" for s in seq), sum(s[1] == "D" for s in seq)
        names = [s[0] for s in seq]

        def unit(cc, name):
            return 5 * cc + names.index(name)

        def freed_upto(u, who):
            if u >= 0:
                return sum(s[1] == who for s in seq[:u + 1])
            return -sum(s[1] == who for s in seq[UB + u + 1:])

        def store_xn(sp, b, cc):
            sp.wait_ge(xn_ok, b * 4 + cc + 3)
            sp.dma_start(d["xn_d"][bass.ds(b, 1), cc * CH:(cc + 1) * CH, :].rearrange(
                "o (t p) m -> p (o t) m", p=P), xn[cc % 2][:, :, :]).then_inc(xn_out[cc % 2], 16)

        def store_parts(sp, b, cc):
            sp.wait_ge(third_ok, b * 18 + 4 * cc + 5)
            p = cc % 2
            for n, dst in (("q", "qp_d"), ("k", "kp_d")):
                for i in range(3):
                    sp.dma_start(d[dst][i, bass.ds(b * DM, DM), cc * CH:(cc + 1) * CH].rearrange(
                        "(f p) t -> p f t", p=P), part[n][p][:, i, :, :]).then_inc(part_out[p], 16)

        def d_v(b, cc, t2):
            return big["V"][:, bass.ds(b * H, H), 4 * cc + 2 * t2:4 * cc + 2 * t2 + 2, :].rearrange("p h t e -> p t h e")

        def put_v(copy, dst, src):
            return copy(dst, src[:, :].rearrange("p (t h e) -> p t h e", t=2, h=H))

        def dve_last(dve, i, b):
            i.then_inc(rest_ok, 1)
            dve.wait_ge(rest_ok, b * 18 + 19)
            dve.sem_inc(freed["D"], 1)
            dve.wait_ge(ring_full, b * UB + UB)
            dve.tensor_copy(big["V"][:, bass.ds(b * H, H), NT, :],
                            bank[1][:, 0:DM].rearrange("p (h e) -> p h e", h=H)).then_inc(freed["D"], 1)

        landed = {e: sem(f"a_landed_{e}") for e in "PDT"}
        blk = ctx.enter_context(nc.Block())

        @blk.sync
        def _(sp):
            sp.dma_start(ident[:, :], d["ident_f"]).then_inc(const_in, 16)
            for n in "qkv":
                sp.dma_start(W[n][:, :, :], d["W" + n].rearrange("(k p) n -> p k n", p=P)).then_inc(const_in, 16)
            sp.dma_start(WR[:, :, :], d["wg"].rearrange("(k p) n -> p k n", p=P)).then_inc(const_in, 16)
            sp.wait_ge(zeroed, 2)
            for h in range(8):
                rows = slice(D * h, D * h + D)
                sp.dma_start(WG[rows, :], d["Wg"]).then_inc(const_in, 16)
                sp.dma_start(WCK[rows, :, rows], d["Wck"].rearrange("(g d) o -> d g o", d=D)).then_inc(const_in, 16)
                sp.dma_start(WCV[rows, :, rows], d["Wcv"].rearrange("(g d) o -> d g o", d=D)).then_inc(const_in, 16)
            with sp.Fori(0, B) as b:
                for cc in range(4):
                    p = cc % 2
                    sp.wait_ge(xn_ok, b * 4 + cc + 1)
                    sp.dma_start(xin[p][:, :, :], d["x"][bass.ds(b, 1), cc * CH:(cc + 1) * CH, :].rearrange(
                        "o (t p) m -> p (o t) m", p=P)).then_inc(x_in[p], 16)
                    if cc >= 1:
                        store_xn(sp, b, cc - 1)
                    if cc >= 2:
                        store_parts(sp, b, cc - 2)
                store_xn(sp, b, 3)
                store_parts(sp, b, 2)
                store_parts(sp, b, 3)
                sp.wait_ge(third_ok, b * 18 + 19)
                for i in range(3):
                    sp.dma_start(d["kp_d"][i, bass.ds(b * DM, DM), T:TK].rearrange("(f p) t -> p f t", p=P),
                                 cpart[:, i, :, :]).then_inc(cpart_out, 16)
            for p in range(2):
                sp.wait_ge(xn_out[p], 16 + 16 * 2 * B)
                sp.wait_ge(part_out[p], 96 + 96 * 2 * B)
            sp.wait_ge(cpart_out, 48 + 48 * B)

        @blk.gpsimd
        def _(pool):
            for p in range(2):
                pool.sem_inc(xn_out[p], 16)
                pool.sem_inc(part_out[p], 96)
            pool.sem_inc(cpart_out, 48)
            pool.sem_inc(third_ok, 1)
            with pool.Fori(0, B) as b:
                for cc in range(4):
                    p = cc % 2
                    for m, (n, f) in enumerate((n, f) for n in "qk" for f in range(2)):
                        pool.wait_ge(rest_ok, b * 18 + 4 * cc + m + 2)
                        if m == 0:
                            pool.wait_ge(part_out[p], b * 192 + 96 * (cc // 2) + 96)
                        land(pool, landed["P"])
                        pool.tensor_copy(part[n][p][:, 1, f, :], rest[n][:, f, :]).then_inc(second_ok, 1)
                        pool.wait_ge(second_ok, b * 18 + 4 * cc + m + 1)
                        pool.tensor_tensor(part[n][p][:, 2, f, :], rest[n][:, f, :], part[n][p][:, 1, f, :],
                                           ALU.subtract).then_inc(third_ok, 1)
                for f in range(2):
                    pool.wait_ge(rest_ok, b * 18 + 18 + f)
                    if f == 0:
                        pool.wait_ge(cpart_out, b * 48 + 48)
                    land(pool, landed["P"])
                    pool.tensor_copy(cpart[:, 1, f, :], crest[:, f, :]).then_inc(second_ok, 1)
                    pool.wait_ge(second_ok, b * 18 + 17 + f)
                    pool.tensor_tensor(cpart[:, 2, f, :], crest[:, f, :], cpart[:, 1, f, :],
                                       ALU.subtract).then_inc(third_ok, 1)

        @blk.scalar
        def _(act):
            act.sem_inc(freed["A"], 2)
            act.sem_inc(std_ok, 1)
            act.wait_ge(zeroed, 3)
            with act.Fori(0, B) as b:
                for cc in range(4):
                    p = cc % 2
                    act.wait_ge(stats, b * 4 + cc + 1)
                    act.wait_ge(rstd_ok, b * 4 + cc + 1)
                    act.activation(std[:, :], mv[:, :, 1], ACT.Sqrt, bias=eps[:, :]).then_inc(std_ok, 1)
                    act.wait_ge(ring_full, b * UB + unit(cc, "xT0") + 1)
                    act.copy(xnT[p][:, 0, :], bank[unit(cc, "xT0") % 2][:, :]).then_inc(freed["A"], 1)
                    for m, (n, f) in enumerate((n, f) for n in "qk" for f in range(2)):
                        act.wait_ge(proj, b * 24 + 6 * cc + m + 1)
                        full = bank[2 + m]
                        if n == "q":
                            act.copy(qT[:, f, :], full[:, :])
                        else:
                            act.copy(kT[:, f, cc * CH:(cc + 1) * CH], full[:, :])
                        act.wait_ge(part_out[p], b * 192 + 96 * (cc // 2) + 96)
                        act.activation(part[n][p][:, 0, f, :], full[:, :], ACT.Copy,
                                       scale=0.25 if n == "q" else 1.0).then_inc(first_ok, 1)
                    act.wait_ge(ring_full, b * UB + unit(cc, "vt0") + 1)
                    put_v(act.copy, d_v(b, cc, 0), bank[unit(cc, "vt0") % 2]).then_inc(freed["A"], 1)
                act.wait_ge(ring_full, b * UB + UB - 1)
                act.wait_ge(cpart_out, b * 48 + 48)
                act.wait_ge(vcT_ok, b + 1)
                for f in range(2):
                    act.copy(cpart[:, 0, f, :], bank[0][:, f * NB:(f + 1) * NB]).then_inc(first_ok, 1)

        @blk.vector
        def _(dve):
            dve.memset(WCK[:, :, :], 0.0).then_inc(zeroed, 1)
            dve.memset(WCV[:, :, :], 0.0).then_inc(zeroed, 1)
            dve.memset(eps[:, :], EPS).then_inc(zeroed, 1)
            dve.sem_inc(freed["D"], 2)
            dve.sem_inc(xn_ok, 2)
            dve.sem_inc(rstd_ok, 1)
            dve.sem_inc(rest_ok, 1)
            dve.sem_inc(vT_ok, 1)
            with dve.Fori(0, B) as b:
                for cc in range(4):
                    p = cc % 2
                    dve.wait_ge(x_in[p], b * 32 + 16 * (cc // 2) + 16)
                    dve.wait_ge(std_ok, b * 4 + cc + 1)
                    for t in range(4):
                        dve.bn_stats(st[:, t, :], xin[p][:, t, :]).then_inc(stats1, 1)
                    dve.wait_ge(stats1, b * 16 + 4 * cc + 4)
                    land(dve, landed["D"])
                    for t in range(4):
                        i = dve.bn_aggr(mv[:, t, :], st[:, t, :])
                    i.then_inc(stats, 1)
                    dve.wait_ge(std_ok, b * 4 + cc + 2)
                    dve.reciprocal(rstd[:, :], std[:, :]).then_inc(rstd_ok, 1)
                    dve.wait_ge(rstd_ok, b * 4 + cc + 2)
                    dve.wait_ge(xn_out[p], b * 32 + 16 * (cc // 2) + 16)
                    for t in range(4):
                        i = dve.tensor_scalar(xn[p][:, t, :], xin[p][:, t, :], mv[:, t, 0:1], rstd[:, t:t + 1],
                                              ALU.subtract, ALU.mult)
                    i.then_inc(xn_ok, 1)
                    dve.wait_ge(ring_full, b * UB + unit(cc, "xT1") + 1)
                    dve.tensor_copy(xnT[p][:, 1, :], bank[unit(cc, "xT1") % 2][:, :]).then_inc(freed["D"], 1)
                    for m, (n, f) in enumerate((n, f) for n in "qk" for f in range(2)):
                        dve.wait_ge(first_ok, b * 18 + 4 * cc + m + 1)
                        dve.wait_ge(third_ok, b * 18 + 4 * cc + 1)
                        dve.scalar_tensor_tensor(rest[n][:, f, :], bank[2 + m][:, :], 0.25 if n == "q" else 1.0,
                                                 part[n][p][:, 0, f, :], ALU.mult, ALU.subtract).then_inc(rest_ok, 1)
                    for f in range(2):
                        dve.wait_ge(proj, b * 24 + 6 * cc + 5 + f)
                        dve.tensor_copy(vT[:, f, cc * CH:(cc + 1) * CH], bank[6 + f][:, :]).then_inc(vT_ok, 1)
                    dve.wait_ge(ring_full, b * UB + unit(cc, "gr") + 1)
                    dve.tensor_copy(big["GL"][:, bass.ds(b * NT + 4 * cc, 4), :],
                                    bank[unit(cc, "gr") % 2][:, 0:4 * 11].rearrange("p (t e) -> p t e", t=4)
                                    ).then_inc(freed["D"], 1)
                    dve.wait_ge(ring_full, b * UB + unit(cc, "vt1") + 1)
                    put_v(dve.tensor_copy, d_v(b, cc, 1), bank[unit(cc, "vt1") % 2]).then_inc(freed["D"], 1)
                dve.wait_ge(ring_full, b * UB + UB - 1)
                dve.tensor_copy(vcT[:, :, :], bank[0][:, 2 * NB:4 * NB].rearrange("p (f n) -> p f n", f=2)).then_inc(vcT_ok, 1)
                for f in range(2):
                    dve.wait_ge(first_ok, b * 18 + 18)
                    dve.wait_ge(third_ok, b * 18 + 17)
                    i = dve.tensor_tensor(crest[:, f, :], bank[0][:, f * NB:(f + 1) * NB], cpart[:, 0, f, :], ALU.subtract)
                    if f == 0:
                        i.then_inc(rest_ok, 1)
                dve_last(dve, i, b)

        @blk.tensor
        def _(pe):
            def ring_wait(b, u):
                if u - 2 >= 0:
                    who = seq[u - 2][1]
                else:
                    who = seq[UB + u - 2][1]
                pe.wait_ge(freed[who], b * (AB if who == "A" else DB) + 2 + freed_upto(u - 2, who))

            pe.wait_ge(const_in, 16 * 29)
            with pe.Fori(0, B) as b:
                for cc in range(4):
                    p = cc % 2
                    pe.wait_ge(xn_ok, b * 4 + cc + 3)
                    for f in range(2):
                        u = unit(cc, f"xT{f}")
                        ring_wait(b, u)
                        for t in range(4):
                            i = pe.transpose(bank[u % 2][:, t * P:(t + 1) * P], xn[p][:, t, f * P:(f + 1) * P], ident[:, :])
                        i.then_inc(ring_full, 1)
                    pe.wait_ge(freed["A"], b * AB + 2 + freed_upto(unit(cc, "xT0"), "A"))
                    pe.wait_ge(freed["D"], b * DB + 2 + freed_upto(unit(cc, "xT1"), "D"))
                    for m, (n, f) in enumerate((n, f) for n in "qkv" for f in range(2)):
                        if m < 4:
                            pe.wait_ge(rest_ok, b * 18 + (4 * cc + m - 3 if cc else 0) + 1)
                        else:
                            pe.wait_ge(vT_ok, b * 8 + 2 * cc + 1)
                        for k in range(2):
                            i = pe.matmul(bank[2 + m][:, :], W[n][:, k, f * P:(f + 1) * P], xnT[p][:, k, :],
                                          start=(k == 0), stop=(k == 1))
                        i.then_inc(proj, 1)
                    u = unit(cc, "gr")
                    ring_wait(b, u)
                    pe.wait_ge(first_ok, b * 18 + 4 * cc + 2)
                    for t in range(4):
                        for f in range(2):
                            pe.matmul(bank[u % 2][:, 11 * t:11 * t + 3], qT[:, f, t * P:(t + 1) * P], WG[:, :],
                                      start=(f == 0 and t == 0), stop=(f == 1), skip_group_check=True)
                        for k in range(2):
                            i = pe.matmul(bank[u % 2][:, 11 * t + 3:11 * t + 11], xnT[p][:, k, t * P:(t + 1) * P],
                                          WR[:, k, :], start=False, stop=(k == 1), skip_group_check=True)
                    i.then_inc(ring_full, 1)
                    pe.wait_ge(vT_ok, b * 8 + 2 * cc + 3)
                    for t2 in range(2):
                        u = unit(cc, f"vt{t2}")
                        ring_wait(b, u)
                        for t in range(2):
                            for f in range(2):
                                i = pe.transpose(bank[u % 2][:, t * DM + f * P:t * DM + (f + 1) * P],
                                                 vT[:, f, cc * CH + (2 * t2 + t) * P:cc * CH + (2 * t2 + t + 1) * P],
                                                 ident[:, :])
                        i.then_inc(ring_full, 1)
                ring_wait(b, UB - 2)
                for w, (src, wt) in enumerate(((kT, WCK), (vT, WCV))):
                    for f in range(2):
                        v = src[:, f, :].rearrange("p (n g) -> p g n", g=G)
                        for g in range(G):
                            i = pe.matmul(bank[0][:, (2 * w + f) * NB:(2 * w + f + 1) * NB], wt[:, g, :], v[:, g, :],
                                          start=(g == 0 and w == 0 and f == 0), stop=(g == G - 1), skip_group_check=True)
                i.then_inc(ring_full, 1)
                ring_wait(b, UB - 1)
                pe.wait_ge(vcT_ok, b + 1)
                for f in range(2):
                    i = pe.transpose(bank[1][:, f * P:(f + 1) * P], vcT[:, f, :], ident[:, :])
                i.then_inc(ring_full, 1)



def phase_r(nc, d, big):
    with ExitStack() as ctx:
        def sb(name, shape, dt=F32):
            return ctx.enter_context(nc.sbuf_tensor(name, shape, dt))

        def sem(name):
            return ctx.enter_context(nc.semaphore(name))

        TT = N // P
        pref = [ctx.enter_context(nc.psum_tensor(f"r_pref{k}", [P, TT, E], F32)) for k in range(2)]
        tot = [ctx.enter_context(nc.psum_tensor(f"r_tot{k}", [P, TT, E], F32)) for k in range(2)]
        bgt = sb("r_bg", [P, 3])
        iota8 = sb("r_iota8", [P, E])
        tri = sb("r_tri", [P, P], BF16)
        ones = sb("r_ones", [P, P], BF16)
        onesf = sb("r_onesf", [P, TT])
        tok2 = sb("r_tok2", [P, TT, 2])
        tokid = sb("r_tokid", [P, TT], I32)
        ga = sb("r_ga", [P, TT, 3])
        gm = sb("r_gm", [P, TT])
        top8 = sb("r_top8", [P, TT, 8])
        idx = sb("r_idx", [P, TT, 8], U32)
        idxf = sb("r_idxf", [P, TT, 2])
        ex = sb("r_ex", [P, TT])
        oh = sb("r_oh", [P, 2, TT, E], BF16)
        incl = sb("r_incl", [P, 2, E, TT])
        rank = sb("r_rank", [P, TT, E])
        pos = sb("r_pos", [P, TT, 2])
        ok = sb("r_ok", [P, TT, 2])
        sc = sb("r_sc", [P, TT, 2])
        zi = sb("r_zi", [P, E * CAP // P], I32)
        si = [sb(f"r_si{i}", [P, 4, 2], I32) for i in range(2)]
        ti = [sb(f"r_ti{i}", [P, 4], I32) for i in range(2)]

        const_in = sem("r_const_in")
        seq = sem("r_seq")
        gates_in = sem("r_gates_in")
        gates_exp = sem("r_gates_exp")
        diff_in = sem("r_diff_in")
        diff_exp = sem("r_diff_exp")
        onehot = sem("r_onehot")
        counted = sem("r_counted")
        zi_ok = sem("r_zi_ok")
        tab_zero = sem("r_tab_zero")
        slots = sem("r_slots")
        si_ok = sem("r_si_ok")
        scat_out = [sem(f"r_scat_out{i}") for i in range(2)]

        landed = {e: sem(f"r_landed_{e}") for e in "PDT"}
        blk = ctx.enter_context(nc.Block())

        @blk.sync
        def _(sp):
            sp.dma_start(bgt[:, :], d["bg"].partition_broadcast(P)).then_inc(const_in, 16)
            sp.dma_start(iota8[:, :], d["iota8"]).then_inc(const_in, 16)
            sp.dma_start(tri[:, :], d["tri"]).then_inc(const_in, 16)
            sp.dma_start(tok2[:, :, :], d["tok2"]).then_inc(const_in, 16)
            sp.dma_start(tokid[:, :], d["tokid"]).then_inc(const_in, 16)
            sp.wait_ge(zi_ok, 1)
            sp.dma_start(d["tab_d"][0:E * CAP, :].rearrange("(p c) o -> p (c o)", p=P), zi[:, :]).then_inc(tab_zero, 16)
            sp.wait_ge(tab_zero, 16)

        @blk.tensor
        def _(pe):
            pe.wait_ge(onehot, 3)
            for k in range(2):
                pe.matmul(pref[k][:, :, :], tri[:, :], oh[:, k, :, :], start=True, stop=True)
                i = pe.matmul(tot[k][:, :, :], ones[:, :], oh[:, k, :, :], start=True, stop=True)
            i.then_inc(counted, 1)

        @blk.scalar
        def _(act):
            act.wait_ge(gates_in, 1)
            act.activation(ga[:, :, :], ga[:, :, :], ACT.Exp).then_inc(gates_exp, 1)
            act.wait_ge(diff_in, 1)
            act.activation(ex[:, :], ex[:, :], ACT.Exp).then_inc(diff_exp, 1)

        @blk.vector
        def _(dve):
            n = [0]

            def chain(ins):
                n[0] += 1
                ins.then_inc(seq, 1)
                dve.wait_ge(seq, n[0])

            GL = big["GL"]
            dve.memset(zi[:, :], 0).then_inc(zi_ok, 1)
            dve.memset(ones[:, :], 1.0).then_inc(onehot, 1)
            dve.memset(onesf[:, :], 1.0)
            dve.wait_ge(const_in, 80)
            chain(dve.scalar_tensor_tensor(ga[:, :, :], GL[:, :, 0:3], 1.0 / H,
                                           bgt[:, :].unsqueeze(1).to_broadcast([P, TT, 3]), ALU.mult, ALU.add))
            chain(dve.tensor_reduce(gm[:, :], ga[:, :, :], AX.X, ALU.max))
            dve.tensor_tensor(ga[:, :, :], ga[:, :, :], gm[:, :].unsqueeze(2).to_broadcast([P, TT, 3]),
                              ALU.subtract).then_inc(gates_in, 1)
            for t in range(TT):
                i = dve.max(top8[:, t, :], GL[:, t, 3:11])
            chain(i)
            for t in range(TT):
                i = dve.max_index(idx[:, t, :], top8[:, t, :], GL[:, t, 3:11])
            chain(i)
            chain(dve.tensor_copy(idxf[:, :, :], idx[:, :, 0:2]))
            for k in range(2):
                i = dve.tensor_tensor(oh[:, k, :, :], iota8[:, :].unsqueeze(1).to_broadcast([P, TT, E]),
                                      idxf[:, :, k:k + 1].to_broadcast([P, TT, E]), ALU.is_equal)
                i.then_inc(onehot, 1)
            dve.tensor_tensor(ex[:, :], top8[:, :, 1], top8[:, :, 0], ALU.subtract).then_inc(diff_in, 1)
            dve.wait_ge(gates_exp, 1)
            chain(dve.tensor_reduce(gm[:, :], ga[:, :, :], AX.X, ALU.add))
            chain(dve.reciprocal(gm[:, :], gm[:, :]))
            chain(dve.tensor_tensor(ga[:, :, :], ga[:, :, :], gm[:, :].unsqueeze(2).to_broadcast([P, TT, 3]), ALU.mult))
            chain(dve.memset(ga[0:G, :, :].rearrange("p (b t) g -> p b t g", b=B)[:, :, 0, 0:1], 0.0))
            for b in range(B):
                for j, br in enumerate((1, 0, 2)):
                    i = dve.tensor_copy(big["gates"][:, b * H:(b + 1) * H, :, j],
                                        ga[:, b * NT:(b + 1) * NT, br].unsqueeze(1).to_broadcast([P, H, NT]))
            chain(i)
            dve.wait_ge(diff_exp, 1)
            chain(dve.tensor_scalar(gm[:, :], ex[:, :], 1.0, None, ALU.add))
            chain(dve.reciprocal(big["gk"][:, :, 0], gm[:, :]))
            chain(dve.tensor_tensor(big["gk"][:, :, 1], ex[:, :], big["gk"][:, :, 0], ALU.mult))
            dve.wait_ge(counted, 1)
            for k in range(2):
                for e in range(E):
                    i = dve.tensor_tensor_scan(out=incl[:, k, e, :], data0=onesf[:, :], data1=tot[k][:, :, e],
                                               initial=incl[:, 0, e, TT - 1:TT] if k else 0.0,
                                               op0=ALU.mult, op1=ALU.add)
                chain(i)
            for k in range(2):
                chain(dve.tensor_tensor(rank[:, :, :], incl[:, k, :, :].rearrange("p e t -> p t e"), pref[k][:, :, :], ALU.add))
                chain(dve.tensor_tensor(rank[:, :, :], rank[:, :, :], tot[k][:, :, :], ALU.subtract))
                chain(dve.tensor_tensor(rank[:, :, :], rank[:, :, :], oh[:, k, :, :], ALU.mult))
                chain(dve.tensor_reduce(pos[:, :, k], rank[:, :, :], AX.X, ALU.add))
            chain(dve.tensor_scalar(ok[:, :, :], pos[:, :, :], float(CAP), None, ALU.is_lt))
            chain(dve.tensor_tensor(big["gk"][:, :, :], big["gk"][:, :, :], ok[:, :, :], ALU.mult))
            chain(dve.tensor_scalar(pos[:, :, :], pos[:, :, :], float(CAP - 1), None, ALU.min))
            chain(dve.scalar_tensor_tensor(pos[:, :, :], idxf[:, :, :], float(CAP), pos[:, :, :], ALU.mult, ALU.add))
            chain(dve.tensor_copy(big["slot"][:, :, :], pos[:, :, :]))
            chain(dve.tensor_tensor(sc[:, :, :], pos[:, :, :], tok2[:, :, :], ALU.subtract))
            chain(dve.tensor_tensor(sc[:, :, :], sc[:, :, :], ok[:, :, :], ALU.mult))
            chain(dve.tensor_tensor(sc[:, :, :], sc[:, :, :], tok2[:, :, :], ALU.add))
            dve.tensor_copy(big["scat"][:, :, :], sc[:, :, :]).then_inc(slots, 1)

        @blk.gpsimd
        def _(pool):
            pool.wait_ge(slots, 1)
            pool.wait_ge(tab_zero, 16)
            with pool.Fori(0, TT // 8) as i:
                for p in range(2):
                    pool.tensor_copy(si[p][:, :, :], big["scat"][:, bass.ds(i * 8 + 4 * p, 4), :]).then_inc(si_ok, 1)
                    pool.tensor_copy(ti[p][:, :], tokid[:, bass.ds(i * 8 + 4 * p, 4)]).then_inc(si_ok, 1)
                    pool.wait_ge(si_ok, i * 4 + 2 * p + 2)
                    land(pool, landed["P"])
                    for t in range(4):
                        for k in range(2):
                            pool.indirect_dma_start(
                                out=d["tab_d"], out_offset=bass.IndirectOffsetOnAxis(ap=si[p][:, t, k:k + 1], axis=0),
                                in_=ti[p][:, t:t + 1], in_offset=None).then_inc(scat_out[p], 16)
                for p in range(2):
                    pool.wait_ge(scat_out[p], i * 128 + 128)


def phase_b(nc, d, big):
    with ExitStack() as ctx:
        def sb(name, shape, dt=F32):
            return ctx.enter_context(nc.sbuf_tensor(name, shape, dt))

        def sem(name):
            return ctx.enter_context(nc.semaphore(name))

        def two(name, shape, dt=F32):
            return [sb(f"b_{name}{i}", shape, dt) for i in range(2)]

        ring = [ctx.enter_context(nc.psum_tensor(f"b_ring{i}", [P, CH], F32)) for i in range(RING)]
        S = [ctx.enter_context(nc.psum_tensor(f"b_scores{i}", [P, CH], F32)) for i in range(SLOTS)]
        accS = ctx.enter_context(nc.psum_tensor("b_acc_sel", [P, CH], F32))
        accB = ctx.enter_context(nc.psum_tensor("b_acc_rest", [P, CH], F32))

        V, gates = big["V"], big["gates"]
        Q = two("q", [P, T], BF16)
        K = two("k", [P, TK], BF16)
        KW = two("kw", [P, T], BF16)
        VH = two("vh", [P, TP, 32])
        PR = two("pr", [P, 4 * CH])
        scs = two("scs", [P, 4, 4 + NB])
        top8 = two("top8", [P, 4, 8])
        rep = two("rep", [P, 4, 4 + NB])
        selm = two("selm", [P, 4, NB], BF16)
        bm = two("bm", [P, 4, NB])
        junk = sb("b_junk", [P, 4, NB])
        mx = two("mx", [P, 4, 3])
        mr = two("mr", [P, 4, 3])
        mp = two("mp", [P, 4, NM], BF16)
        maskT = two("maskT", [P, CH], BF16)
        accS_s = two("accS_s", [P, CH])
        accB_s = two("accB_s", [64, CH])
        rden = sb("b_rden", [P, 4, 3])
        wgt = sb("b_wgt", [P, 4, 3])
        tmp = two("tmp", [P, 4, 3, D])
        att1 = sb("b_att1", [P, 4, D])
        ident = sb("b_ident", [P, P], BF16)
        expand = sb("b_expand", [P, T], BF16)
        cmp_m = sb("b_cmp_m", [P, 4, 32], BF16)
        cmp_m0 = sb("b_cmp_m0", [P, 4, 32], BF16)
        cmp_mT = sb("b_cmp_mT", [P, T], BF16)
        win_m = sb("b_win_m", [P, 2, LW], BF16)
        win_m0 = sb("b_win_m0", [P, 2, LW], BF16)
        win_mT = sb("b_win_mT", [P, WIN + 3 * LW + P], BF16)
        cau = sb("b_cau", [P, P], BF16)
        cauT = sb("b_cauT", [P, P], BF16)
        first4 = sb("b_first4", [P, 8])
        collect = sb("b_collect", [P, 32])
        pick = sb("b_pick", [64, 64])
        zeros = sb("b_zeros", [P, P], BF16)

        const_in = sem("b_const_in")
        filled = sem("b_filled")
        kq_in = [sem(f"b_kq_in{i}") for i in range(2)]
        vh_ok = sem("b_vh_ok")
        ring_full = sem("b_ring_full")
        freed = {"A": sem("b_freed_act"), "D": sem("b_freed_dve")}
        s_full = sem("b_scores_full")
        exp_ok = sem("b_exp_ok")
        pv_ok = sem("b_pv_ok")
        mc0_ok = sem("b_mc0_ok")
        bias_ok = sem("b_bias_ok")
        top_ok = sem("b_top_ok")
        fill_ok = sem("b_fill_ok")
        rep_ok = sem("b_rep_ok")
        selm_ok = sem("b_selm_ok")
        mx_ok = sem("b_mx_ok")
        mp1_ok = sem("b_mp1_ok")
        mr1_ok = sem("b_mr1_ok")
        mp2_ok = sem("b_mp2_ok")
        mr2_ok = sem("b_mr2_ok")
        mp_ok = sem("b_mp_ok")
        maxrow_full = sem("b_maxrow_full")
        maxrow_ok = sem("b_maxrow_ok")
        accS_ok = sem("b_accS_ok")
        accB_ok = sem("b_accB_ok")
        rden_ok = sem("b_rden_ok")
        wgt_ok = sem("b_wgt_ok")
        tmp_ok = sem("b_tmp_ok")
        att1_ok = sem("b_att1_ok")
        att_ok = sem("b_att_ok")

        consts = [("ident_b", ident), ("expand", expand), ("cmp_m", cmp_m), ("cmp_m0", cmp_m0), ("cmp_mT", cmp_mT), ("win_m", win_m),
                  ("win_m0", win_m0), ("win_mT", win_mT), ("cau", cau), ("cauT", cauT), ("first4", first4),
                  ("collect", collect), ("pick", pick)]

        consts_total = 16 * (len(consts) + 4)

        def body_starts(i):
            return dict(step=i * (2 * NC), unit=i * (2 * UNITS_H), group=i * (2 * GROUPS_H), head=i * 2,
                        ru=i * RU, ra=i * RA, rd=i * RD, i=i)

        landed = {e: sem(f"b_landed_{e}") for e in "PDT"}
        blk = ctx.enter_context(nc.Block())

        @blk.sync
        def _(sp):
            for n, t in consts:
                sp.dma_start(t[:], d[n]).then_inc(const_in, 16)
            for p in range(2):
                sp.dma_start(K[p][QK:ROWS, :], d["k_ones"]).then_inc(const_in, 16)
                sp.dma_start(KW[p][QK:ROWS, :], d["kw_ones"]).then_inc(const_in, 16)

            def load(head, p):
                for r, (a, b) in enumerate(((0, 0), (0, 1), (0, 2), (1, 0), (1, 1), (2, 0))):
                    rows = slice(D * r, D * r + D)
                    sp.dma_start(Q[p][rows, :], d["qp_d"][a, bass.ds(head * D, D), :]).then_inc(kq_in[p], 16)
                    sp.dma_start(K[p][rows, :], d["kp_d"][b, bass.ds(head * D, D), :]).then_inc(kq_in[p], 16)
                    sp.dma_start(KW[p][rows, :], d["kp_d"][b, bass.ds(head * D, D), 0:T]).then_inc(kq_in[p], 16)

            load(0, 0)
            load(1, 1)
            with sp.Fori(0, BH // 2 - 1) as i:
                for p in range(2):
                    sp.wait_ge(pv_ok, i * (2 * GROUPS_H) + GROUPS_H * (p + 1) + 2)
                    load(i * 2 + 2 + p, p)

        LOADS = 18 * 16

        def sel_rows(c):
            return slice(64, 96) if c == 0 else slice(0, P)

        @blk.tensor
        def _(pe):
            def form_ring(kind, r, kk, c, p, mpar, u, before, n, first_load=None):
                out = ring[u % RING]
                if before is not None:
                    who, k = before
                    pe.wait_ge(freed[who], (n["ra"] if who == "A" else n["rd"]) + k)
                q0 = c * CH
                if kind == "scs":
                    if first_load is not None:
                        pe.wait_ge(kq_in[p], first_load)
                    ov = out[:, :].rearrange("p (t n) -> p t n", t=4)
                    pe.matmul(ov[:, :, 32 * c:32 * c + 32], ident[:, :], (cmp_m if c else cmp_m0)[:, :, :], start=True, stop=False,
                              skip_group_check=True)
                    for t in range(4):
                        i = pe.matmul(ov[:, t, 0:32 * (c + 1)], Q[p][0:QK, q0 + t * P:q0 + (t + 1) * P],
                                      K[p][0:QK, T:T + 32 * (c + 1)], start=False, stop=True, skip_group_check=True)
                elif kind == "loc":
                    m = win_m0 if c == 0 and r == 0 else win_m
                    ov = out[:, 0:2 * LW].rearrange("p (t n) -> p t n", t=2)
                    pe.matmul(ov, ident[:, :], m[:, :, :], start=True, stop=False, skip_group_check=True)
                    for t in range(2):
                        tile = 4 * c + 2 * r + t
                        lo = WIN if tile == 0 else 0
                        i = pe.matmul(ov[:, t, lo:LW], Q[p][0:QK, tile * P:(tile + 1) * P],
                                      K[p][0:QK, tile * P - WIN + lo:tile * P + P], start=False, stop=True,
                                      skip_group_check=True)
                elif kind == "S":
                    w = CH if kk < c else P * (r + 1)
                    edge = c == 0 and r == 0
                    i = pe.matmul(out[:, 0:w], Q[p][0:QK, q0 + r * P:q0 + (r + 1) * P],
                                  K[p][0:QK, kk * CH:kk * CH + w], start=True, stop=not edge)
                    if edge:
                        i = pe.matmul(out[:, 0:w], ident[:, :], cau[:, :], start=False, stop=True)
                elif kind == "maskT":
                    nb = 32 * (c + 1)
                    pe.wait_ge(selm_ok, n["next"] + 1)
                    land(pe, landed["T"])
                    ob = out[:, :].bitcast(BF16)
                    for t in range(4):
                        i = pe.transpose(ob[0:nb, t * P:(t + 1) * P], selm[mpar][:, t, 0:nb], ident[:, :])
                else:
                    pe.wait_ge(accS_ok, n["s"] + 2)
                    pe.wait_ge(accB_ok, n["s"] + 2)
                    ov = out[:, :].rearrange("p (t n) -> p t n", t=4)
                    rows = sel_rows(c)
                    for t in range(4):
                        pe.matmul(ov[:, t, 0:32], accS_s[mpar][rows, t * P:(t + 1) * P], collect[rows, :],
                                  start=(t == 0), stop=True, skip_group_check=True)
                        i = pe.matmul(ov[:, t, 32:96], accB_s[mpar][:, t * P:(t + 1) * P], pick[:, :],
                                      start=False, stop=True, skip_group_check=True)
                i.then_inc(ring_full, 1)

            def max_rows(step, par):
                pe.wait_ge(mp_ok, step + 1)
                pe.wait_ge(maxrow_ok, step + 1)
                for t in range(4):
                    i = pe.matmul(accB[QK:ROWS, t * P:(t + 1) * P], mp[par][:, t, :], ident[:, :],
                                  start=True, stop=True, tile_position=(0, QK), skip_group_check=True)
                i.then_inc(maxrow_full, 1)

            def scores(c, u, slot, at_once, p, par, unit):
                pe.wait_ge(exp_ok, unit + (SLOTS if at_once else 1))
                for segs in banks_of(c)[u:u + 1]:
                    out = S[slot]
                    q0 = c * CH
                    if segs[0][0] == "L":
                        i = pe.matmul(out[:, :], ident[:, :], win_mT[:, 0:CH], start=True, stop=False, skip_group_check=True)
                    for si_, (kind, j, q, w, at) in enumerate(segs):
                        qs = Q[p][0:ROWS, q0 + q:q0 + q + w]
                        o = out[:, at:at + w]
                        if kind == "C":
                            pe.matmul(o, K[p][0:ROWS, T:TK], qs, start=True, stop=False, skip_group_check=True)
                            i = pe.matmul(o, ident[:, :], cmp_mT[:, q0:q0 + CH], start=False, stop=True, skip_group_check=True)
                        elif kind == "L":
                            if segs[0][0] != "L":
                                pe.matmul(o, ident[:, :], win_mT[:, CH:CH + P], start=False, stop=False, skip_group_check=True)
                            i = pe.matmul(o, KW[p][0:ROWS, j * P:(j + 1) * P], qs, start=False, stop=True, skip_group_check=True)
                        else:
                            pe.matmul(o, K[p][0:ROWS, j * P:(j + 1) * P], qs, start=(si_ == 0), stop=False, skip_group_check=True)
                            i = pe.matmul(o, expand[:, j * P:(j + 1) * P], maskT[par][:, q:q + w], start=False, stop=True,
                                          skip_group_check=True)
                            if c == 0 and j == 0:
                                i = pe.matmul(out[:, 0:P], ident[:, :], cauT[:, :], start=False, stop=True, skip_group_check=True)
                i.then_inc(s_full, 1)

            def values(c, g, p, unit_end, gpar, started):
                pe.wait_ge(exp_ok, unit_end + SLOTS)
                for pos, segs in enumerate(banks_of(c)[4 * g:4 * g + 4]):
                    for kind, j, q, w, at in segs:
                        pr = PR[gpar][:, pos * CH + at:pos * CH + at + w]
                        if kind == "S":
                            col = 32 * pos if c else 64
                            out = accS[col:col + 32, q:q + w]
                        elif kind == "C":
                            out, col = accB[0:32, q:q + w], 0
                        else:
                            out, col = accB[32:64, q:q + w], 32
                        start = (kind, col) not in started
                        started.add((kind, col))
                        i = pe.matmul(out, VH[p][:, j, :], pr, start=start, stop=False, tile_position=(0, col),
                                      skip_group_check=True)
                i.then_inc(pv_ok, 1)

            def step(n, ls, last):
                c, hp, p, par = chunk_of(ls), ls // NC, ls // NC % 2, ls % 2
                nls = ls + 1
                nxt = None if last else chunk_of(nls)
                s = n["step"] + ls
                u0, g0 = unit_before(ls), group_before(ls)
                started = set()
                for it in step_plan(c, nxt, ls == 0):
                    if it[0] == "ring":
                        _, kind, r, kk = it
                        u, before = rg.next(kind)
                        if kind == "out":
                            form_ring(kind, r, kk, chunk_of(ls - 1), p, (ls - 1) % 2, u, before, dict(n, s=s - 1))
                        else:
                            need = None
                            if kind == "scs" and nls % NC == 0:
                                need = (n["i"] + 1 + nls // (2 * NC)) * LOADS
                            form_ring(kind, r, kk, nxt, nls // NC % 2, nls % 2, u, before, dict(n, next=s + 1), need)
                    elif it[0] == "maxrows":
                        max_rows(s + 1, nls % 2)
                    elif it[0] == "scores":
                        u = it[1]
                        if u == 0:
                            pe.wait_ge(maxrow_ok, s + 2)
                        scores(c, u, *slot_of(ls, u), p, par, n["unit"] + u0 + u)
                    else:
                        g = it[1]
                        if g == 0:
                            if ls % NC == 0:
                                pe.wait_ge(vh_ok, n["head"] + hp + 1)
                            pe.wait_ge(accS_ok, s + 1)
                            pe.wait_ge(accB_ok, s + 1)
                            land(pe, landed["T"])
                        last_u = min(4 * g + 3, units_of(c) - 1)
                        values(c, g, p, n["unit"] + u0 + last_u + 1, (g0 + g) % 2, started)

            pe.wait_ge(const_in, consts_total)
            pe.wait_ge(filled, 1)
            pe.sem_inc(pv_ok, 2)
            rg = Ring()
            n0 = dict(body_starts(0), next=0)
            for kind, r, kk in PRO:
                u, before = rg.next(kind)
                form_ring(kind, r, kk, 0, 0, 0, u, before, n0, LOADS if kind == "scs" else None)
            max_rows(0, 0)
            step(n0, 0, False)
            with pe.Fori(0, BH // 2 - 1) as i:
                rg = ring_at_body()
                for ls in range(1, 2 * NC + 1):
                    step(body_starts(i), ls, False)
            rg = ring_at_body()
            for ls in range(1, 2 * NC):
                step(body_starts(BH // 2 - 1), ls, ls == 2 * NC - 1)
            u, before = rg.next("out")
            form_ring("out", 0, 0, chunk_of(2 * NC - 1), 1, 1, u, before, dict(body_starts(BH // 2 - 1), s=BH * NC - 1))

        @blk.scalar
        def _(act):
            def ring_unit(kind, c, p, par, u, n, step):
                act.wait_ge(ring_full, n["ru"] + u + 1)
                out = ring[u % RING]
                if kind == "scs":
                    act.wait_ge(rep_ok, step + 1)
                    act.copy(scs[par][:, :, 4:4 + 32 * (c + 1)],
                             out[:, :].rearrange("p (t n) -> p t n", t=4)[:, :, 0:32 * (c + 1)]).then_inc(freed["A"], 1)
                else:
                    nb = 32 * (c + 1)
                    act.copy(maskT[par][0:nb, :], out[0:nb, :].bitcast(BF16)[:, 0:CH]).then_inc(freed["A"], 1)

            def max_rows(c, p, step):
                act.wait_ge(maxrow_full, step + 1)
                act.copy(Q[p][QK:ROWS, c * CH:(c + 1) * CH], accB[QK:ROWS, :]).then_inc(maxrow_ok, 1)

            def step(n, ls, last):
                c, par, nls = chunk_of(ls), ls % 2, ls + 1
                nxt = None if last else chunk_of(nls)
                np_ = nls // NC % 2
                s = n["step"] + ls
                u0, g0 = unit_before(ls), group_before(ls)
                for it in step_plan(c, nxt, ls == 0):
                    if it[0] == "ring":
                        u, _ = rg.next(it[1])
                        if it[1] in ("scs", "maskT"):
                            ring_unit(it[1], nxt, np_, nls % 2, u, n, s + 1)
                    elif it[0] == "maxrows":
                        max_rows(nxt, np_, s + 1)
                    elif it[0] == "scores":
                        u = it[1]
                        g = u // 4
                        w = max(seg[4] + seg[3] for seg in banks_of(c)[u])
                        act.wait_ge(s_full, n["unit"] + u0 + u + 1)
                        if u % 4 == 0:
                            act.wait_ge(pv_ok, n["group"] + g0 + g + 1)
                        at = (u % 4) * CH
                        act.activation(PR[(g0 + g) % 2][:, at:at + w], S[slot_of(ls, u)[0]][:, 0:w], ACT.Exp).then_inc(exp_ok, 1)
                act.wait_ge(pv_ok, n["group"] + g0 + c + 2 + 2)
                act.copy(accB_s[par][:, :], accB[0:64, :]).then_inc(accB_ok, 1)

            act.sem_inc(exp_ok, SLOTS)
            act.sem_inc(accB_ok, 1)
            act.sem_inc(maxrow_ok, 1)
            rg = Ring()
            n0 = body_starts(0)
            for kind, r, kk in PRO:
                u, _ = rg.next(kind)
                if kind in ("scs", "maskT"):
                    ring_unit(kind, 0, 0, 0, u, n0, 0)
            max_rows(0, 0, 0)
            step(n0, 0, False)
            with act.Fori(0, BH // 2 - 1) as i:
                rg = ring_at_body()
                for ls in range(1, 2 * NC + 1):
                    step(body_starts(i), ls, False)
            rg = ring_at_body()
            for ls in range(1, 2 * NC):
                step(body_starts(BH // 2 - 1), ls, ls == 2 * NC - 1)

        @blk.vector
        def _(dve):
            def reduce_unit(kind, r, kk, c, par, u, n):
                dve.wait_ge(ring_full, n["ru"] + u + 1)
                out = ring[u % RING]
                if kind == "loc":
                    dve.tensor_reduce(mx[par][:, 2 * r:2 * r + 2, 2], out[:, 0:2 * LW].rearrange("p (t n) -> p t n", t=2),
                                      AX.X, ALU.max).then_inc(freed["D"], 1)
                else:
                    w = CH if kk < c else P * (r + 1)
                    dve.tensor_reduce(bm[par][:, r, 32 * kk:32 * kk + w // G],
                                      out[:, 0:w].rearrange("p (n g) -> p n g", g=G), AX.X, ALU.max).then_inc(freed["D"], 1)

            def choose(c, par, step, head, scs_count):
                nb = 32 * (c + 1)
                dve.wait_ge(freed["A"], scs_count)
                if c == 0:
                    dve.tensor_reduce(mx[par][:, 0, 1:2], scs[par][:, 0, 4:12], AX.X, ALU.max)
                    dve.tensor_tensor(scs[par][:, 0, 4:12], scs[par][:, 0, 4:12], first4[:, :], ALU.add).then_inc(bias_ok, 1)
                    dve.wait_ge(bias_ok, head + 1)
                land(dve, landed["D"])
                for t in range(4):
                    i = dve.max(top8[par][:, t, :], scs[par][:, t, 4:4 + nb])
                i.then_inc(top_ok, 1)

            def mark(c, par, step):
                nb = 32 * (c + 1)
                dve.wait_ge(top_ok, step + 1)
                lo = 1 if c == 0 else 0
                dve.tensor_copy(mx[par][:, lo:4, 1], top8[par][:, lo:4, 0])
                dve.memset(top8[par][:, :, 4:8], FAR).then_inc(fill_ok, 1)
                dve.wait_ge(fill_ok, step + 1)
                land(dve, landed["D"])
                for t in range(4):
                    i = dve.match_replace(rep[par][:, t, 0:4 + nb], top8[par][:, t, :], scs[par][:, t, 0:4 + nb], FOUND)
                i.then_inc(rep_ok, 1)

            def maxima(c, par, step, reduced):
                dve.wait_ge(selm_ok, step + 1)
                dve.wait_ge(freed["D"], reduced)
                land(dve, landed["D"])
                for t in range(4):
                    nb = 8 * (4 * c + t + 1)
                    i = dve.tensor_tensor_reduce(out=junk[:, t, 0:nb], in0=bm[par][:, t, 0:nb], in1=selm[par][:, t, 0:nb],
                                                 scale=1.0, scalar=FAR, op0=ALU.add, op1=ALU.max,
                                                 accum_out=mx[par][:, t, 0:1])
                i.then_inc(mx_ok, 1)
                parts = mp[par][:, :, :].rearrange("p t (b i) -> p t b i", i=3)
                dve.wait_ge(mx_ok, step + 1)
                dve.tensor_scalar(parts[:, :, :, 0], mx[par][:, :, :], -1.0, None, ALU.mult).then_inc(mp1_ok, 1)
                dve.wait_ge(mp1_ok, step + 1)
                dve.scalar_tensor_tensor(mr[par][:, :, :], mx[par][:, :, :], -1.0, parts[:, :, :, 0], ALU.mult,
                                         ALU.subtract).then_inc(mr1_ok, 1)
                dve.wait_ge(mr1_ok, step + 1)
                dve.tensor_copy(parts[:, :, :, 1], mr[par][:, :, :]).then_inc(mp2_ok, 1)
                dve.wait_ge(mp2_ok, step + 1)
                dve.tensor_tensor(parts[:, :, :, 2], mr[par][:, :, :], parts[:, :, :, 1], ALU.subtract).then_inc(mp_ok, 1)

            def results(c, hp, par, u, n, s):
                dve.wait_ge(ring_full, n["ru"] + u + 1)
                ov = ring[u % RING][:, :].rearrange("p (t n) -> p t n", t=4)[:, :, 0:96].rearrange("p t (b e) -> p t b e", b=3)
                dve.reciprocal(rden[:, :, :], ov[:, :, :, D]).then_inc(rden_ok, 1)
                dve.wait_ge(rden_ok, s + 1)
                dve.tensor_tensor(wgt[:, :, :].unsqueeze(1), rden[:, :, :].unsqueeze(1),
                                  gates[:, bass.ds(n["head"] + hp, 1), 4 * c:4 * c + 4, :], ALU.mult).then_inc(wgt_ok, 1)
                dve.wait_ge(wgt_ok, s + 1)
                dve.wait_ge(att_ok, s + 1)
                dve.tensor_tensor(tmp[par][:, :, :, :], ov[:, :, :, 0:D],
                                  wgt[:, :, :].unsqueeze(3).to_broadcast([P, 4, 3, D]), ALU.mult).then_inc(freed["D"], 1)

            def step(n, ls, last):
                c, par, nls = chunk_of(ls), ls % 2, ls + 1
                nxt = None if last else chunk_of(nls)
                s = n["step"] + ls
                scs_count, seen = None, 0
                g0 = group_before(ls)
                for it in step_plan(c, nxt, ls == 0):
                    if it[0] == "ring":
                        _, kind, r, kk = it
                        u, _ = rg.next(kind)
                        if kind == "scs":
                            scs_count = n["ra"] + rg.owners[-1][1]
                        elif kind in ("loc", "S"):
                            reduce_unit(kind, r, kk, nxt, nls % 2, u, n)
                        elif kind == "out":
                            results(chunk_of(ls - 1), (ls - 1) // NC, (ls - 1) % 2, u, n, s - 1)
                        seen += 1
                        if nxt is not None and seen == AT_TOP:
                            choose(nxt, nls % 2, s + 1, n["head"] + nls // NC, scs_count)
                        if nxt is not None and seen == AT_FOUND:
                            mark(nxt, nls % 2, s + 1)
                    elif it[0] == "maxrows":
                        maxima(nxt, nls % 2, s + 1, n["rd"] + rg.freed["D"])
                dve.wait_ge(pv_ok, n["group"] + g0 + c + 2 + 2)
                dve.tensor_copy(accS_s[par][sel_rows(c), :], accS[sel_rows(c), :]).then_inc(accS_ok, 1)

            for p in range(2):
                dve.memset(VH[p][:, :, D + 1:32], 0.0)
                dve.memset(VH[p][:, :, D:D + 1], 1.0)
                dve.memset(scs[p][:, :, 0:4], FAR)
                dve.memset(maskT[p][:, :], 0.0)
            dve.memset(zeros[:, :], 0.0).then_inc(filled, 1)
            dve.sem_inc(rep_ok, 2)
            dve.sem_inc(accS_ok, 1)
            dve.wait_ge(const_in, consts_total)
            rg = Ring()
            n0 = body_starts(0)
            for kind, r, kk in PRO:
                u, _ = rg.next(kind)
                if kind == "scs":
                    scs_count = rg.owners[-1][1]
                elif kind in ("loc", "S"):
                    reduce_unit(kind, r, kk, 0, 0, u, n0)
            choose(0, 0, 0, 0, scs_count)
            mark(0, 0, 0)
            maxima(0, 0, 0, rg.freed["D"])
            step(n0, 0, False)
            with dve.Fori(0, BH // 2 - 1) as i:
                rg = ring_at_body()
                for ls in range(1, 2 * NC + 1):
                    step(body_starts(i), ls, False)
            rg = ring_at_body()
            for ls in range(1, 2 * NC):
                step(body_starts(BH // 2 - 1), ls, ls == 2 * NC - 1)
            u, _ = rg.next("out")
            results(chunk_of(2 * NC - 1), 1, 1, u, body_starts(BH // 2 - 1), BH * NC - 1)

        @blk.gpsimd
        def _(pool):
            def values_of(head, p):
                land(pool, landed["P"])
                pool.tensor_copy(VH[p][:, :, 0:D].unsqueeze(1), V[:, bass.ds(head, 1), :, :]).then_inc(vh_ok, 1)

            def masks(c, par, step):
                nb = 32 * (c + 1)
                pool.wait_ge(rep_ok, step + 3)
                land(pool, landed["P"])
                pool.tensor_scalar(selm[par][:, :, 0:nb], rep[par][:, :, 4:4 + nb], 1.0e38, NEG, ALU.is_lt,
                                   ALU.mult).then_inc(selm_ok, 1)

            def sum_up(ls, n):
                c, hp, par, s = chunk_of(ls), ls // NC, ls % 2, n["step"] + ls
                pool.wait_ge(freed["D"], n["rd"] + rg.freed["D"])
                pool.wait_ge(att_ok, s + 2)
                pool.tensor_tensor(att1[:, :, :], tmp[par][:, :, 0, :], tmp[par][:, :, 1, :], ALU.add).then_inc(att1_ok, 1)
                pool.wait_ge(att1_ok, s + 1)
                pool.wait_ge(vh_ok, n["head"] + hp + 1)
                pool.tensor_tensor(V[:, bass.ds(n["head"] + hp, 1), 4 * c:4 * c + 4, :], att1[:, :, :].unsqueeze(1),
                                   tmp[par][:, :, 2, :].unsqueeze(1), ALU.add).then_inc(att_ok, 1)

            def step(n, ls, last):
                c, hp = chunk_of(ls), ls // NC
                nxt = None if last else chunk_of(ls + 1)
                s = n["step"] + ls
                for it in step_plan(c, nxt, ls == 0):
                    if it[0] != "ring":
                        continue
                    rg.next(it[1])
                    if it[1] == "maskT":
                        masks(nxt, (ls + 1) % 2, s + 1)
                    elif it[1] == "out":
                        sum_up(ls - 1, n)
                if ls % NC == NC - 1 and not n.get("tail"):
                    pool.wait_ge(pv_ok, n["group"] + GROUPS_H * (hp + 1) + 2)
                    values_of(n["head"] + hp + 2, hp % 2)

            pool.wait_ge(filled, 1)
            pool.sem_inc(att_ok, 2)
            values_of(0, 0)
            values_of(1, 1)
            rg = Ring()
            for kind, _, _ in PRO:
                rg.next(kind)
            masks(0, 0, 0)
            step(body_starts(0), 0, False)
            with pool.Fori(0, BH // 2 - 1) as i:
                rg = ring_at_body()
                for ls in range(1, 2 * NC + 1):
                    step(body_starts(i), ls, False)
            rg = ring_at_body()
            for ls in range(1, 2 * NC):
                step(dict(body_starts(BH // 2 - 1), tail=True), ls, ls == 2 * NC - 1)
            rg.next("out")
            sum_up(2 * NC - 1, body_starts(BH // 2 - 1))


def phase_c(nc, d):
    with ExitStack() as ctx:
        def two(name, shape, dt=F32):
            return [ctx.enter_context(nc.sbuf_tensor(f"c_{name}{i}", shape, dt)) for i in range(2)]

        def sem(name):
            return ctx.enter_context(nc.semaphore(name))

        bank = [ctx.enter_context(nc.psum_tensor(f"c_bank{i}", [P, CH], F32)) for i in range(8)]
        ident = ctx.enter_context(nc.sbuf_tensor("c_ident", [P, P], F32))
        w1 = two("w1", [P, 2, HID])
        w2 = two("w2", [P, HID // P, DM])
        b1 = two("b1", [P, HID // P])
        b2 = two("b2", [P, DM])
        ids = two("ids", [P, CAP // P], I32)
        xg = two("xg", [P, 4, DM])
        xT = two("xT", [P, 2, CH])
        hT = two("hT", [P, HID // P, CH])
        ys = two("ys", [P, 4, DM])
        NM8 = HID // P

        ident_in = sem("c_ident_in")
        w_in = [sem(f"c_w_in{i}") for i in range(2)]
        x_in = [sem(f"c_x_in{i}") for i in range(2)]
        turned = sem("c_turned")
        xT0_ok, xT1_ok = sem("c_xT0_ok"), sem("c_xT1_ok")
        h_full, h_ok = sem("c_h_full"), sem("c_h_ok")
        y_full, y_ok = sem("c_y_full"), sem("c_y_ok")
        y_out = [sem(f"c_y_out{i}") for i in range(2)]

        def load_next(sp, load, i):
            load(((i * 2) + 2) % E, 0)

        landed = {e: sem(f"c_landed_{e}") for e in "PDT"}
        blk = ctx.enter_context(nc.Block())

        @blk.sync
        def _(sp):
            sp.dma_start(ident[:, :], d["ident_f"]).then_inc(ident_in, 16)

            def load(e, p):
                sp.dma_start(w1[p][:, :, :].unsqueeze(1), d["w1"][bass.ds(e, 1)].rearrange("e (k p) n -> p e k n", p=P)).then_inc(w_in[p], 16)
                sp.dma_start(w2[p][:, :, :].unsqueeze(1), d["w2"][bass.ds(e, 1)].rearrange("e (k p) n -> p e k n", p=P)).then_inc(w_in[p], 16)
                sp.dma_start(b1[p][:, :].unsqueeze(1), d["b1"][bass.ds(e, 1)].rearrange("e (k p) -> p e k", p=P),
                             allow_slow_non_contiguous=True).then_inc(w_in[p], 16)
                sp.dma_start(b2[p][:, :], d["b2"][bass.ds(e, 1)].to_broadcast([P, DM])).then_inc(w_in[p], 16)
                sp.dma_start(ids[p][:, :], d["tab_d"][bass.ds(e * CAP, CAP), :].rearrange("(p t) o -> p (t o)", p=P)).then_inc(w_in[p], 16)

            load(0, 0)
            with sp.Fori(0, E // 2) as i:
                for p in range(2):
                    for cc in range(4):
                        k = 4 * p + cc
                        if cc == 1:
                            if p == 0:
                                load(i * 2 + 1, 1)
                            else:
                                load_next(sp, load, i)
                        sp.wait_ge(y_ok, i * 16 + 2 * k + 4)
                        sp.dma_start(d["y_d"][bass.ds((i * 2 + p) * CAP, CAP), :].rearrange(
                            "(p t) m -> p t m", p=P)[:, 4 * cc:4 * cc + 4, :],
                                     ys[k % 2][:, :, :]).then_inc(y_out[k % 2], 16)
            for p in range(2):
                sp.wait_ge(y_out[p], 16 + 16 * E * 2)

        @blk.gpsimd
        def _(pool):
            pool.sem_inc(y_out[0], 16)
            pool.sem_inc(y_out[1], 16)
            with pool.Fori(0, E // 2) as i:
                for p in range(2):
                    pool.wait_ge(w_in[p], i * 80 + 80)
                    for cc in range(4):
                        k = 4 * p + cc
                        pool.wait_ge(turned, i * 16 + 2 * k + 1)
                        land(pool, landed["P"])
                        for t in range(4):
                            pool.indirect_dma_start(
                                out=xg[k % 2][:, t, :], out_offset=None, in_=d["xn_d"].rearrange("b t m -> (b t) m"),
                                in_offset=bass.IndirectOffsetOnAxis(ap=ids[p][:, 4 * cc + t:4 * cc + t + 1], axis=0)
                            ).then_inc(x_in[k % 2], 16)

        @blk.tensor
        def _(pe):
            pe.wait_ge(ident_in, 16)
            pe.sem_inc(turned, 3)
            with pe.Fori(0, E // 2) as i:
                for p in range(2):
                    pe.wait_ge(w_in[p], i * 80 + 80)
                    for cc in range(4):
                        k = 4 * p + cc
                        pe.wait_ge(x_in[k % 2], i * 256 + 64 * (k // 2) + 64)
                        pe.wait_ge(xT0_ok, i * 8 + k + 1)
                        pe.wait_ge(xT1_ok, i * 8 + k + 1)
                        for f in range(2):
                            for t in range(4):
                                m = pe.transpose(bank[f][:, t * P:(t + 1) * P], xg[k % 2][:, t, f * P:(f + 1) * P], ident[:, :])
                            m.then_inc(turned, 1)
                        pe.wait_ge(xT0_ok, i * 8 + k + 2)
                        pe.wait_ge(xT1_ok, i * 8 + k + 2)
                        for j in range(NM8):
                            pe.wait_ge(h_ok, i * 64 + 8 * k + j + 1)
                            for f in range(2):
                                m = pe.matmul(bank[2 + j % 4][:, :], w1[p][:, f, j * P:(j + 1) * P], xT[k % 2][:, f, :],
                                              start=(f == 0), stop=(f == 1))
                            m.then_inc(h_full, 1)
                        for t2 in range(2):
                            pe.wait_ge(y_ok, i * 16 + 2 * k + t2 + 1)
                            if t2 == 0:
                                pe.wait_ge(h_ok, i * 64 + 8 * k + 8 + 4)
                            for t in range(2):
                                for j in range(NM8):
                                    m = pe.matmul(bank[6 + t2][:, t * DM:(t + 1) * DM],
                                                  hT[k % 2][:, j, (2 * t2 + t) * P:(2 * t2 + t + 1) * P], w2[p][:, j, :],
                                                  start=(j == 0), stop=(j == NM8 - 1), skip_group_check=True)
                            m.then_inc(y_full, 1)

        @blk.scalar
        def _(act):
            act.sem_inc(h_ok, 4)
            act.sem_inc(xT0_ok, 1)
            with act.Fori(0, E // 2) as i:
                for p in range(2):
                    for cc in range(4):
                        k = 4 * p + cc
                        act.wait_ge(turned, i * 16 + 2 * k + 4)
                        act.copy(xT[k % 2][:, 0, :], bank[0][:, :]).then_inc(xT0_ok, 1)
                        act.wait_ge(w_in[p], i * 80 + 80)
                        for j in range(NM8):
                            act.wait_ge(h_full, i * 64 + 8 * k + j + 1)
                            act.activation(hT[k % 2][:, j, :], bank[2 + j % 4][:, :], ACT.Relu,
                                           bias=b1[p][:, j:j + 1]).then_inc(h_ok, 1)

        @blk.vector
        def _(dve):
            dve.sem_inc(xT1_ok, 1)
            dve.sem_inc(y_ok, 2)
            with dve.Fori(0, E // 2) as i:
                for p in range(2):
                    for cc in range(4):
                        k = 4 * p + cc
                        dve.wait_ge(turned, i * 16 + 2 * k + 5)
                        dve.tensor_copy(xT[k % 2][:, 1, :], bank[1][:, :]).then_inc(xT1_ok, 1)
                        dve.wait_ge(w_in[p], i * 80 + 80)
                        for t2 in range(2):
                            dve.wait_ge(y_full, i * 16 + 2 * k + t2 + 1)
                            dve.wait_ge(y_out[k % 2], i * 64 + 16 * (k // 2) + 16)
                            dve.tensor_tensor(ys[k % 2][:, 2 * t2:2 * t2 + 2, :],
                                              bank[6 + t2][:, :].rearrange("p (t m) -> p t m", t=2),
                                              b2[p][:, :].unsqueeze(1).to_broadcast([P, 2, DM]), ALU.add).then_inc(y_ok, 1)


def phase_d(nc, d, big):
    with ExitStack() as ctx:
        def two(name, shape, dt=F32):
            return [ctx.enter_context(nc.sbuf_tensor(f"d_{name}{i}", shape, dt)) for i in range(2)]

        def sem(name):
            return ctx.enter_context(nc.semaphore(name))

        bank = [ctx.enter_context(nc.psum_tensor(f"d_bank{i}", [P, CH], F32)) for i in range(4)]
        ident = ctx.enter_context(nc.sbuf_tensor("d_ident", [P, P], F32))
        Wo = ctx.enter_context(nc.sbuf_tensor("d_Wo", [P, 2, DM], F32))
        xs = two("xs", [P, 4, DM])
        y = [two(f"y{k}", [P, 4, DM]) for k in range(2)]
        att = two("att", [P, 4, H, D])
        attT = two("attT", [P, 2, CH])
        si = two("si", [P, 4, 2], I32)
        gs = two("gs", [P, 4, 2])
        res = two("res", [P, 4, DM])

        const_in = sem("d_const_in")
        x_in = [sem(f"d_x_in{i}") for i in range(2)]
        y_in = [sem(f"d_y_in{i}") for i in range(2)]
        att_ok, si_ok = sem("d_att_ok"), sem("d_si_ok")
        turned, aT0_ok, aT1_ok = sem("d_turned"), sem("d_aT0_ok"), sem("d_aT1_ok")
        o_full, o_ok = sem("d_o_full"), sem("d_o_ok")
        r1_ok, r2_ok = sem("d_r1_ok"), sem("d_r2_ok")
        out_done = [sem(f"d_out_done{i}") for i in range(2)]

        def store(sp, b, cc):
            sp.wait_ge(r2_ok, b * 4 + cc + 3)
            sp.dma_start(d["out"][bass.ds(b, 1), cc * CH:(cc + 1) * CH, :].rearrange("o (t p) m -> p (o t) m", p=P),
                         res[cc % 2][:, :, :]).then_inc(out_done[cc % 2], 16)

        landed = {e: sem(f"d_landed_{e}") for e in "PDT"}
        blk = ctx.enter_context(nc.Block())

        @blk.sync
        def _(sp):
            sp.dma_start(ident[:, :], d["ident_f"]).then_inc(const_in, 16)
            sp.dma_start(Wo[:, :, :], d["Wo"].rearrange("(k p) n -> p k n", p=P)).then_inc(const_in, 16)
            sp.sem_inc(out_done[0], 16)
            sp.sem_inc(out_done[1], 16)
            with sp.Fori(0, B) as b:
                for cc in range(4):
                    p = cc % 2
                    sp.wait_ge(r2_ok, b * 4 + cc + 1)
                    sp.dma_start(xs[p][:, :, :], d["x"][bass.ds(b, 1), cc * CH:(cc + 1) * CH, :].rearrange(
                        "o (t p) m -> p (o t) m", p=P)).then_inc(x_in[p], 16)
                    if cc:
                        store(sp, b, cc - 1)
                store(sp, b, 3)
            for p in range(2):
                sp.wait_ge(out_done[p], 16 + 16 * B * 2)

        @blk.gpsimd
        def _(pool):
            with pool.Fori(0, B) as b:
                for cc in range(4):
                    p = cc % 2
                    pool.wait_ge(r2_ok, b * 4 + cc + 1)
                    land(pool, landed["P"])
                    pool.tensor_copy(si[p][:, :, :], big["slot"][:, bass.ds(b * NT + 4 * cc, 4), :]).then_inc(si_ok, 1)
                    pool.tensor_copy(gs[p][:, :, :], big["gk"][:, bass.ds(b * NT + 4 * cc, 4), :]).then_inc(si_ok, 1)
                    pool.wait_ge(si_ok, b * 8 + 2 * cc + 2)
                    land(pool, landed["P"])
                    for t in range(4):
                        for k in range(2):
                            pool.indirect_dma_start(out=y[k][p][:, t, :], out_offset=None, in_=d["y_d"],
                                                    in_offset=bass.IndirectOffsetOnAxis(ap=si[p][:, t, k:k + 1], axis=0)
                                                    ).then_inc(y_in[p], 16)

        @blk.tensor
        def _(pe):
            pe.wait_ge(const_in, 32)
            pe.sem_inc(turned, 1)
            with pe.Fori(0, B) as b:
                for cc in range(4):
                    p = cc % 2
                    pe.wait_ge(att_ok, b * 4 + cc + 1)
                    pe.wait_ge(aT0_ok, b * 4 + cc + 1)
                    pe.wait_ge(aT1_ok, b * 4 + cc + 1)
                    for f in range(2):
                        for t in range(4):
                            m = pe.transpose(bank[f][:, t * P:(t + 1) * P],
                                             att[p][:, t, 8 * f:8 * f + 8, :].rearrange("p h e -> p (h e)"), ident[:, :])
                        m.then_inc(turned, 1)
                    pe.wait_ge(aT0_ok, b * 4 + cc + 2)
                    pe.wait_ge(aT1_ok, b * 4 + cc + 2)
                    pe.wait_ge(o_ok, b * 8 + 2 * cc + 1)
                    for t2 in range(2):
                        for t in range(2):
                            for f in range(2):
                                m = pe.matmul(bank[2 + t2][:, t * DM:(t + 1) * DM],
                                              attT[p][:, f, (2 * t2 + t) * P:(2 * t2 + t + 1) * P], Wo[:, f, :],
                                              start=(f == 0), stop=(f == 1), skip_group_check=True)
                        m.then_inc(o_full, 1)

        @blk.scalar
        def _(act):
            act.sem_inc(aT0_ok, 1)
            with act.Fori(0, B) as b:
                for cc in range(4):
                    act.wait_ge(turned, b * 8 + 2 * cc + 1)
                    act.copy(att[cc % 2][:, :, :, :], big["V"][:, bass.ds(b * H, H), 4 * cc:4 * cc + 4, :].rearrange(
                        "p h t e -> p t h e")).then_inc(att_ok, 1)
                    act.wait_ge(turned, b * 8 + 2 * cc + 2)
                    act.copy(attT[cc % 2][:, 0, :], bank[0][:, :]).then_inc(aT0_ok, 1)

        @blk.vector
        def _(dve):
            dve.sem_inc(r2_ok, 2)
            dve.sem_inc(aT1_ok, 1)
            dve.sem_inc(o_ok, 1)
            with dve.Fori(0, B) as b:
                for cc in range(4):
                    p = cc % 2
                    dve.wait_ge(turned, b * 8 + 2 * cc + 3)
                    dve.tensor_copy(attT[p][:, 1, :], bank[1][:, :]).then_inc(aT1_ok, 1)
                    dve.wait_ge(x_in[p], b * 32 + 16 * (cc // 2) + 16)
                    dve.wait_ge(out_done[p], b * 32 + 16 * (cc // 2) + 16)
                    for t2 in range(2):
                        dve.wait_ge(o_full, b * 8 + 2 * cc + t2 + 1)
                        dve.tensor_tensor(res[p][:, 2 * t2:2 * t2 + 2, :], bank[2 + t2][:, :].rearrange("p (t m) -> p t m", t=2),
                                          xs[p][:, 2 * t2:2 * t2 + 2, :], ALU.add).then_inc(o_ok, 1)
                    dve.wait_ge(o_ok, b * 8 + 2 * cc + 3)
                    dve.wait_ge(y_in[p], b * 256 + 128 * (cc // 2) + 128)
                    for t in range(4):
                        m = dve.scalar_tensor_tensor(res[p][:, t, :], y[0][p][:, t, :], gs[p][:, t, 0:1], res[p][:, t, :],
                                                     ALU.mult, ALU.add)
                    m.then_inc(r1_ok, 1)
                    dve.wait_ge(r1_ok, b * 4 + cc + 1)
                    for t in range(4):
                        m = dve.scalar_tensor_tensor(res[p][:, t, :], y[1][p][:, t, :], gs[p][:, t, 1:2], res[p][:, t, :],
                                                     ALU.mult, ALU.add)
                    m.then_inc(r2_ok, 1)


def build(nc, d, upto="D"):
    TT = N // P
    with ExitStack() as ctx:
        def sb(name, shape, dt=F32):
            return ctx.enter_context(nc.sbuf_tensor(name, shape, dt))

        big = {
            "V": sb("V", [P, BH, TP, D]),
            "gates": sb("gates", [P, BH, NT, 3]),
            "GL": sb("GL", [P, TT, 3 + E]),
            "gk": sb("gk", [P, TT, 2]),
            "slot": sb("slot", [P, TT, 2], I32),
            "scat": sb("scat", [P, TT, 2], I32),
        }
        phase_a(nc, d, big)
        phase_r(nc, d, big)
        phase_b(nc, d, big)
        phase_c(nc, d)
        phase_d(nc, d, big)


def constants():
    import numpy as np

    def bf(a):
        return (np.ascontiguousarray(a, dtype=np.float32).view(np.uint32) >> 16).astype(np.uint16)

    p, q = np.arange(P)[:, None], np.arange(P)[None, :]

    def mask(bad):
        return bf(np.where(bad, NEG, 0.0))

    t, n = np.arange(T), np.arange(NB)
    cmp_m = np.stack([mask(P * r + p < G * (np.arange(32)[None, :] + 1)) for r in range(4)], 1)
    cmp_m0 = np.stack([mask(np.maximum(P * r + p, G) < G * (np.arange(32)[None, :] + 1)) for r in range(4)], 1)
    y = np.arange(LW)[None, :]
    win = mask((y < p) | (y > p + WIN))
    win0 = mask((y < p) | (y > p + WIN) | (y < WIN))
    winT = mask((y < p) | (y > p + WIN))
    before = mask((np.arange(WIN)[None, :] + P - p) > WIN)
    sel = np.zeros((P, 32), np.float32)
    for g in range(4):
        sel[32 * g + np.arange(32), np.arange(32)] = 1.0
    k_ones = np.zeros((NM, TK), np.float32)
    k_ones[0:3, :T] = 1.0
    k_ones[3:6, T:] = 1.0
    kw_ones = np.zeros((NM, T), np.float32)
    kw_ones[6:9] = 1.0
    tile = np.arange(N // P)
    return {
        "ident_f": np.eye(P, dtype=np.float32),
        "ident_b": bf(np.eye(P)),
        "tri": bf(p < q),
        "iota8": np.tile(np.arange(E, dtype=np.float32), (P, 1)),
        "tok2": (E * CAP + 2.0 * (tile[None, :, None] * P + p[:, :, None]) + np.arange(2)[None, None, :]).astype(np.float32),
        "tokid": (tile[None, :] * P + p).astype(np.int32),
        "expand": bf(t[None, :] // G == n[:, None]),
        "cmp_m": cmp_m,
        "cmp_m0": cmp_m0,
        "cmp_mT": mask(np.maximum(t, G)[None, :] < G * (n[:, None] + 1)),
        "win_m": np.stack([win, win], 1),
        "win_m0": np.stack([win0, win], 1),
        "win_mT": np.concatenate([before, winT, winT, winT, winT[:, :P]], 1),
        "cau": mask(q > p),
        "cauT": mask(p > q),
        "first4": np.where((p < 64) & (np.arange(8)[None, :] < 4), 2.0 ** 32, 0.0).astype(np.float32),
        "collect": sel,
        "pick": np.eye(64, dtype=np.float32),
        "k_ones": bf(k_ones),
        "kw_ones": bf(kw_ones),
    }


NAMES = {"L0_attn_x": "x", "L0_attn_Wq": "Wq", "L0_attn_Wk": "Wk", "L0_attn_Wv": "Wv", "L0_attn_Wo": "Wo",
         "L0_attn_Wck": "Wck", "L0_attn_Wcv": "Wcv", "L0_attn_Wg": "Wg", "L0_attn_bg": "bg", "L0_ffn_wg": "wg",
         "L0_ffn_w1": "w1", "L0_ffn_b1": "b1", "L0_ffn_w2": "w2", "L0_ffn_b2": "b2"}


def kernel(**inputs):
    import concourse.bacc as bacc
    import numpy as np
    from concourse.bass_utils import run_bass_kernel_spmd

    nc = bacc.Bacc("TRN2", target_bir_lowering=False, num_devices=1)
    arrays, d = {}, {}
    for name, short in NAMES.items():
        arrays[f"in_{short}"] = np.ascontiguousarray(inputs[name])
        d[short] = arrays[f"in_{short}"]
    for name, a in constants().items():
        arrays[f"const_{name}"] = np.ascontiguousarray(a)
        d[name] = arrays[f"const_{name}"]
    for name, a in list(d.items()):
        prefix = "in_" if f"in_{name}" in arrays else "const_"
        d[name] = nc.dram_tensor(prefix + name, a.shape, mybir.dt.from_np(a.dtype), kind="ExternalInput").ap()
        if a.dtype == np.uint16:
            d[name] = d[name].bitcast(BF16)
    d["out"] = nc.dram_tensor("out_0", (B, T, DM), F32, kind="ExternalOutput").ap()
    d["xn_d"] = nc.dram_tensor("xn_d", (B, T, DM), F32, kind="Internal").ap()
    d["qp_d"] = nc.dram_tensor("qp_d", (3, B * DM, T), BF16, kind="Internal").ap()
    d["kp_d"] = nc.dram_tensor("kp_d", (3, B * DM, TK), BF16, kind="Internal").ap()
    d["tab_d"] = nc.dram_tensor("tab_d", (2 * E * CAP, 1), I32, kind="Internal").ap()
    d["y_d"] = nc.dram_tensor("y_d", (E * CAP, DM), F32, kind="Internal").ap()
    build(nc, d)
    return run_bass_kernel_spmd(nc, [arrays], core_ids=[0]).results[0]["out_0"]
```

```python
from contextlib import ExitStack

import concourse.bass as bass
from concourse import mybir

F32 = mybir.dt.float32
BF16 = mybir.dt.bfloat16
I32 = mybir.dt.int32
U32 = mybir.dt.uint32
ALU = mybir.AluOpType
ACT = mybir.ActivationFunctionType
AX = mybir.AxisListType

P = 128
B, T, DM = 4, 2048, 256
H, D = 16, 16
G = 16
NB = T // G
NT = T // P
CH = 512
NC = T // CH
BH = B * H
TK = T + NB
QK = 6 * D
NM = 9
ROWS = QK + NM
WIN = 32
LW = P + WIN
E, KTOP, HID = 8, 2, 1024
N = B * T
CAP = KTOP * N // E
NEG = -(2.0 ** 30)
FAR = -3.0e38
FOUND = 3.0e38
EPS = 1e-5
TP = NT + 1


def banks_of(c):
    t = 4 * c
    window = [("L", t - 1, 0, WIN, 0)] if c else []
    window += [("L", t + r, P * r, LW, WIN + LW * r) for r in range(3)]
    return ([[("C", NT, 0, CH, 0)], window, [("S", t, 0, CH, 0)],
             [("S", t + 1, P, 3 * P, 0), ("S", t + 3, 3 * P, P, 3 * P)]]
            + [[("S", j, 0, CH, 0)] for j in range(t)]
            + [[("S", t + 2, 2 * P, 2 * P, 0), ("L", t + 3, 3 * P, P, 2 * P)]])


def ahead_of(c):
    return ([("scs", 0, 0), ("loc", 0, 0), ("loc", 1, 0)]
            + [("S", r, kk) for r in range(4) for kk in range(c + 1)])


SEQ = list(range(NC)) + list(range(NC))[::-1]


def chunk_of(ls):
    return SEQ[ls % (2 * NC)]


def units_of(c):
    return 4 * c + 5


def ring_cost(kind, kk, c):
    if kind == "S":
        return 560 if kk < c else 380
    return {"scs": 500, "loc": 420}[kind]


def step_plan(c, nxt, first=False):
    base = []
    for u in range(units_of(c)):
        base.append(("scores", u))
        if u % 4 == 1 and u > 4:
            base.append(("values", u // 4 - 1))
    base.append(("values", c))
    ahead = ahead_of(nxt) if nxt is not None else []
    cost = {"scores": 430, "values": 900}
    room = sum(cost[b[0]] for b in base) - TAIL
    need, t = [], START
    for n_, (kind, r, kk) in enumerate(ahead):
        t += ring_cost(kind, kk, nxt) + (CHOOSE if n_ + 1 in (AT_TOP, AT_FOUND) else 0)
        need.append(t)
    total = need[-1] if need else 1
    scale = min(1.0, room / total)
    order, pe, done = [], 0, 0
    for item in base:
        while done < len(ahead) and (need[done - RING] * scale if done >= RING else done * FIRST) <= pe:
            order.append(("ring",) + ahead[done])
            done += 1
        order.append(item)
        pe += cost[item[0]]
    tail = order.pop()
    order += [("ring",) + a for a in ahead[done:]]
    if nxt is not None:
        order.append(("ring", "maskT", 0, 0))
    if not first:
        order.append(("ring", "out", 0, 0))
    order.append(tail)
    if nxt is not None:
        order.append(("maxrows",))
    order.append(("values", c + 1))
    return order


START, CHOOSE, TAIL, FIRST = 300, 600, 400, 0


AT_TOP, AT_FOUND = 3, 5
RING = 3
SLOTS = 3
CONSUMER = {"scs": "A", "loc": "D", "S": "D", "maskT": "A", "out": "D"}


class Ring:

    def __init__(self):
        self.unit, self.freed, self.owners = 0, {"A": 0, "D": 0}, []

    def next(self, kind):
        before = self.owners[-RING] if len(self.owners) >= RING else None
        u = self.unit
        self.unit += 1
        self.freed[CONSUMER[kind]] += 1
        self.owners.append((CONSUMER[kind], self.freed[CONSUMER[kind]]))
        return u, before

    def through(self, steps):
        for ls in steps:
            for it in step_plan(chunk_of(ls), chunk_of(ls + 1), ls == 0):
                if it[0] == "ring":
                    self.next(it[1])
        return self


PRO = ahead_of(0) + [("maskT", 0, 0)]


def ring_at_body():
    r = Ring()
    for kind, _, _ in PRO:
        r.next(kind)
    r.through([0])
    r.owners = ([("D", r.freed["D"] - k) for k in range(RING - 2, 0, -1)]
                + [("A", r.freed["A"]), ("D", r.freed["D"])])
    return r


def ring_per_body():
    a, b = ring_at_body(), ring_at_body().through(range(1, 2 * NC + 1))
    return b.unit - a.unit, b.freed["A"] - a.freed["A"], b.freed["D"] - a.freed["D"]


RU, RA, RD = ring_per_body()
assert RU % RING == 0
UNITS_H = sum(units_of(c) for c in range(NC))
GROUPS_H = sum(c + 2 for c in range(NC))


def unit_before(ls):
    return sum(units_of(chunk_of(x)) for x in range(ls))


def slot_of(ls, u):
    v = unit_before(ls if ls else 2 * NC) - units_of(0) + u
    return v % SLOTS, v == 0 and (2 * UNITS_H - 1) % SLOTS == 0


def group_before(ls):
    return sum(chunk_of(x) + 2 for x in range(ls))


def land(eng, sem):
    eng.sem_inc(sem, 1)


def phase_a(nc, d, big):
    with ExitStack() as ctx:
        def sb(name, shape, dt=F32):
            return ctx.enter_context(nc.sbuf_tensor(name, shape, dt))

        def sem(name):
            return ctx.enter_context(nc.semaphore(name))

        bank = [ctx.enter_context(nc.psum_tensor(f"a_bank{i}", [P, CH], F32)) for i in range(8)]
        ident = sb("a_ident", [P, P])
        W = {n: sb(f"a_w{n}", [P, 2, DM]) for n in "qkv"}
        WCK = sb("a_wck", [P, G, P])
        WCV = sb("a_wcv", [P, G, P])
        WG = sb("a_wgate", [P, 3])
        WR = sb("a_wrouter", [P, 2, E])
        eps = sb("a_eps", [P, 1])
        xin = [sb(f"a_xin{i}", [P, 4, DM]) for i in range(2)]
        xn = [sb(f"a_xn{i}", [P, 4, DM]) for i in range(2)]
        xnT = [sb(f"a_xnT{i}", [P, 2, CH]) for i in range(2)]
        st = sb("a_st", [P, 4, 6])
        mv = sb("a_mv", [P, 4, 2])
        std = sb("a_std", [P, 4])
        rstd = sb("a_rstd", [P, 4])
        qT = sb("a_qT", [P, 2, CH])
        kT = sb("a_kT", [P, 2, T])
        vT = sb("a_vT", [P, 2, T])
        part = {n: [sb(f"a_{n}part{i}", [P, 3, 2, CH], BF16) for i in range(2)] for n in "qk"}
        rest = {n: sb(f"a_{n}rest", [P, 2, CH]) for n in "qk"}
        cpart = sb("a_cpart", [P, 3, 2, NB], BF16)
        crest = sb("a_crest", [P, 2, NB])
        vcT = sb("a_vcT", [P, 2, NB])

        const_in = sem("a_const_in")
        diag_in = sem("a_diag_in")
        zeroed = sem("a_zeroed")
        x_in = [sem(f"a_x_in{i}") for i in range(2)]
        xn_out = [sem(f"a_xn_out{i}") for i in range(2)]
        part_out = [sem(f"a_part_out{i}") for i in range(2)]
        cpart_out = sem("a_cpart_out")
        stats1 = sem("a_stats1")
        stats = sem("a_stats")
        std_ok = sem("a_std_ok")
        rstd_ok = sem("a_rstd_ok")
        xn_ok = sem("a_xn_ok")
        ring_full = sem("a_ring_full")
        freed = {"A": sem("a_freed_act"), "D": sem("a_freed_dve")}
        proj = sem("a_proj")
        first_ok = sem("a_first_ok")
        rest_ok = sem("a_rest_ok")
        vT_ok = sem("a_vT_ok")
        second_ok = sem("a_second_ok")
        third_ok = sem("a_third_ok")
        c1_ok = sem("a_c1_ok")
        vcT_ok = sem("a_vcT_ok")

        owner = {"xT0": "A", "xT1": "D", "gr": "D", "vt0": "A", "vt1": "D", "kcvc": "D", "vcT": "D"}

        def units(last):
            out = []
            for cc in range(4):
                if not (last and cc == 3):
                    out += [("xT0", cc + 1), ("xT1", cc + 1)]
                out += [("gr", cc), ("vt0", cc), ("vt1", cc)]
            return out + [("kcvc", 0), ("vcT", 0)]

        UB = len(units(False))
        AB = sum(owner[n] == "A" for n, _ in units(False))
        DB = UB - AB

        def full_count(b, name, cc, last):
            return b * UB + 2 + units(last).index((name, cc)) + 1

        def ring_bank(name, cc, last):
            return bank[units(last).index((name, cc)) % 2]

        def freed_count(b, who, upto, last):
            return b * (AB if who == "A" else DB) + 3 + sum(owner[n] == who for n, _ in units(last)[:upto])

        def store_xn(sp, b, cc):
            sp.wait_ge(xn_ok, b * 4 + cc + 3)
            sp.dma_start(d["xn_d"][bass.ds(b, 1), cc * CH:(cc + 1) * CH, :].rearrange(
                "o (t p) m -> p (o t) m", p=P), xn[cc % 2][:, :, :]).then_inc(xn_out[cc % 2], 16)

        def store_parts(sp, b, cc):
            sp.wait_ge(third_ok, b * 18 + 4 * cc + 5)
            p = cc % 2
            for n, dst in (("q", "qp_d"), ("k", "kp_d")):
                for i in range(3):
                    sp.dma_start(d[dst][i, bass.ds(b * DM, DM), cc * CH:(cc + 1) * CH].rearrange(
                        "(f p) t -> p f t", p=P), part[n][p][:, i, :, :]).then_inc(part_out[p], 16)

        def d_v(b, cc, t2):
            return big["V"][:, bass.ds(b * H, H), 4 * cc + 2 * t2:4 * cc + 2 * t2 + 2, :].rearrange("p h t e -> p t h e")

        def put_v(copy, dst, src):
            return copy(dst, src[:, :].rearrange("p (t h e) -> p t h e", t=2, h=H))

        landed = {e: sem(f"a_landed_{e}") for e in "PDT"}
        blk = ctx.enter_context(nc.Block())

        @blk.sync
        def _(sp):
            def load(b, cc):
                sp.dma_start(xin[cc % 2][:, :, :], d["x"][bass.ds(b + cc // 4, 1), cc % 4 * CH:(cc % 4 + 1) * CH, :].rearrange(
                    "o (t p) m -> p (o t) m", p=P)).then_inc(x_in[cc % 2], 16)

            load(0, 0)
            sp.dma_start(ident[:, :], d["ident_f"]).then_inc(const_in, 16)
            for n in "qkv":
                sp.dma_start(W[n][:, :, :], d["W" + n].rearrange("(k p) n -> p k n", p=P)).then_inc(const_in, 16)
            sp.dma_start(WR[:, :, :], d["wg"].rearrange("(k p) n -> p k n", p=P)).then_inc(const_in, 16)
            load(0, 1)
            sp.wait_ge(zeroed, 2)
            for h in range(8):
                rows = slice(D * h, D * h + D)
                sp.dma_start(WG[rows, :], d["Wg"]).then_inc(diag_in, 16)
                sp.dma_start(WCK[rows, :, rows], d["Wck"].rearrange("(g d) o -> d g o", d=D)).then_inc(diag_in, 16)
                sp.dma_start(WCV[rows, :, rows], d["Wcv"].rearrange("(g d) o -> d g o", d=D)).then_inc(diag_in, 16)

            def batch(b, last):
                for cc in range(4):
                    store_xn(sp, b, cc)
                    if not (last and cc >= 2):
                        load(b, cc + 2)
                    if cc >= 1:
                        store_parts(sp, b, cc - 1)
                store_parts(sp, b, 3)
                sp.wait_ge(third_ok, b * 18 + 19)
                for i in range(3):
                    sp.dma_start(d["kp_d"][i, bass.ds(b * DM, DM), T:TK].rearrange("(f p) t -> p f t", p=P),
                                 cpart[:, i, :, :]).then_inc(cpart_out, 16)

            with sp.Fori(0, B - 1) as b:
                batch(b, False)
            batch(B - 1, True)
            for p in range(2):
                sp.wait_ge(xn_out[p], 16 + 16 * 2 * B)
                sp.wait_ge(part_out[p], 96 + 96 * 2 * B)
            sp.wait_ge(cpart_out, 48 + 48 * B)

        @blk.gpsimd
        def _(pool):
            for p in range(2):
                pool.sem_inc(xn_out[p], 16)
                pool.sem_inc(part_out[p], 96)
            pool.sem_inc(cpart_out, 48)
            pool.sem_inc(third_ok, 1)
            with pool.Fori(0, B) as b:
                for cc in range(4):
                    p = cc % 2
                    for m, (n, f) in enumerate((n, f) for n in "qk" for f in range(2)):
                        pool.wait_ge(rest_ok, b * 18 + 4 * cc + m + 2)
                        if m == 0:
                            pool.wait_ge(part_out[p], b * 192 + 96 * (cc // 2) + 96)
                        land(pool, landed["P"])
                        pool.tensor_copy(part[n][p][:, 1, f, :], rest[n][:, f, :]).then_inc(second_ok, 1)
                        pool.wait_ge(second_ok, b * 18 + 4 * cc + m + 1)
                        pool.tensor_tensor(part[n][p][:, 2, f, :], rest[n][:, f, :], part[n][p][:, 1, f, :],
                                           ALU.subtract).then_inc(third_ok, 1)
                for f in range(2):
                    pool.wait_ge(rest_ok, b * 18 + 18 + f)
                    if f == 0:
                        pool.wait_ge(cpart_out, b * 48 + 48)
                    land(pool, landed["P"])
                    pool.tensor_copy(cpart[:, 1, f, :], crest[:, f, :]).then_inc(second_ok, 1)
                    pool.wait_ge(second_ok, b * 18 + 17 + f)
                    pool.tensor_tensor(cpart[:, 2, f, :], crest[:, f, :], cpart[:, 1, f, :],
                                       ALU.subtract).then_inc(third_ok, 1)

        @blk.scalar
        def _(act):
            act.sem_inc(freed["A"], 2)
            act.sem_inc(std_ok, 1)
            act.wait_ge(zeroed, 3)

            def deviation(k):
                act.wait_ge(stats, k + 1)
                act.wait_ge(rstd_ok, k + 1)
                act.activation(std[:, :], mv[:, :, 1], ACT.Sqrt, bias=eps[:, :]).then_inc(std_ok, 1)

            def batch(b, last):
                for cc in range(4):
                    p = cc % 2
                    ahead = not (last and cc == 3)
                    if ahead:
                        deviation(b * 4 + cc + 1)
                    for m, (n, f) in enumerate((n, f) for n in "qk" for f in range(2)):
                        act.wait_ge(proj, b * 24 + 6 * cc + m + 1)
                        full = bank[2 + m]
                        if n == "q":
                            act.copy(qT[:, f, :], full[:, :])
                        else:
                            act.copy(kT[:, f, cc * CH:(cc + 1) * CH], full[:, :])
                        act.wait_ge(part_out[p], b * 192 + 96 * (cc // 2) + 96)
                        act.activation(part[n][p][:, 0, f, :], full[:, :], ACT.Copy,
                                       scale=0.25 if n == "q" else 1.0).then_inc(first_ok, 1)
                    if ahead:
                        act.wait_ge(ring_full, full_count(b, "xT0", cc + 1, last))
                        act.copy(xnT[1 - p][:, 0, :], ring_bank("xT0", cc + 1, last)[:, :]).then_inc(freed["A"], 1)
                    act.wait_ge(ring_full, full_count(b, "vt0", cc, last))
                    put_v(act.copy, d_v(b, cc, 0), ring_bank("vt0", cc, last)).then_inc(freed["A"], 1)
                act.wait_ge(ring_full, full_count(b, "kcvc", 0, last))
                act.wait_ge(cpart_out, b * 48 + 48)
                act.wait_ge(vcT_ok, b + 1)
                for f in range(2):
                    act.copy(cpart[:, 0, f, :], bank[0][:, f * NB:(f + 1) * NB]).then_inc(first_ok, 1)

            deviation(0)
            act.wait_ge(ring_full, 1)
            act.copy(xnT[0][:, 0, :], bank[0][:, :]).then_inc(freed["A"], 1)
            with act.Fori(0, B - 1) as b:
                batch(b, False)
            batch(B - 1, True)

        @blk.vector
        def _(dve):
            dve.memset(WCK[:, :, :], 0.0).then_inc(zeroed, 1)
            dve.memset(WCV[:, :, :], 0.0).then_inc(zeroed, 1)
            dve.memset(eps[:, :], EPS).then_inc(zeroed, 1)
            dve.sem_inc(freed["D"], 2)
            dve.sem_inc(xn_ok, 2)
            dve.sem_inc(rstd_ok, 1)
            dve.sem_inc(rest_ok, 1)
            dve.sem_inc(vT_ok, 1)

            def normalise(b, cc):
                k, p = b * 4 + cc, cc % 2
                dve.wait_ge(x_in[p], b * 32 + 16 * (cc // 2) + 16)
                dve.wait_ge(std_ok, k + 1)
                for t in range(4):
                    dve.bn_stats(st[:, t, :], xin[p][:, t, :]).then_inc(stats1, 1)
                dve.wait_ge(stats1, k * 4 + 4)
                land(dve, landed["D"])
                for t in range(4):
                    i = dve.bn_aggr(mv[:, t, :], st[:, t, :])
                i.then_inc(stats, 1)
                dve.wait_ge(std_ok, k + 2)
                dve.reciprocal(rstd[:, :], std[:, :]).then_inc(rstd_ok, 1)
                dve.wait_ge(rstd_ok, k + 2)
                dve.wait_ge(xn_out[p], b * 32 + 16 * (cc // 2) + 16)
                for t in range(4):
                    i = dve.tensor_scalar(xn[p][:, t, :], xin[p][:, t, :], mv[:, t, 0:1], rstd[:, t:t + 1],
                                          ALU.subtract, ALU.mult)
                i.then_inc(xn_ok, 1)

            def batch(b, last):
                for cc in range(4):
                    p = cc % 2
                    ahead = not (last and cc == 3)
                    if ahead:
                        normalise(b, cc + 1)
                    for m, (n, f) in enumerate((n, f) for n in "qk" for f in range(2)):
                        dve.wait_ge(first_ok, b * 18 + 4 * cc + m + 1)
                        dve.wait_ge(third_ok, b * 18 + 4 * cc + 1)
                        dve.scalar_tensor_tensor(rest[n][:, f, :], bank[2 + m][:, :], 0.25 if n == "q" else 1.0,
                                                 part[n][p][:, 0, f, :], ALU.mult, ALU.subtract).then_inc(rest_ok, 1)
                    for f in range(2):
                        dve.wait_ge(proj, b * 24 + 6 * cc + 5 + f)
                        dve.tensor_copy(vT[:, f, cc * CH:(cc + 1) * CH], bank[6 + f][:, :]).then_inc(vT_ok, 1)
                    if ahead:
                        dve.wait_ge(ring_full, full_count(b, "xT1", cc + 1, last))
                        dve.tensor_copy(xnT[1 - p][:, 1, :], ring_bank("xT1", cc + 1, last)[:, :]).then_inc(freed["D"], 1)
                    dve.wait_ge(ring_full, full_count(b, "gr", cc, last))
                    dve.tensor_copy(big["GL"][:, bass.ds(b * NT + 4 * cc, 4), :],
                                    ring_bank("gr", cc, last)[:, 0:4 * 11].rearrange("p (t e) -> p t e", t=4)
                                    ).then_inc(freed["D"], 1)
                    dve.wait_ge(ring_full, full_count(b, "vt1", cc, last))
                    put_v(dve.tensor_copy, d_v(b, cc, 1), ring_bank("vt1", cc, last)).then_inc(freed["D"], 1)
                dve.wait_ge(ring_full, full_count(b, "kcvc", 0, last))
                dve.tensor_copy(vcT[:, :, :], bank[0][:, 2 * NB:4 * NB].rearrange("p (f n) -> p f n", f=2)).then_inc(vcT_ok, 1)
                for f in range(2):
                    dve.wait_ge(first_ok, b * 18 + 18)
                    dve.wait_ge(third_ok, b * 18 + 17)
                    dve.tensor_tensor(crest[:, f, :], bank[0][:, f * NB:(f + 1) * NB], cpart[:, 0, f, :],
                                      ALU.subtract).then_inc(rest_ok, 1)
                dve.wait_ge(rest_ok, b * 18 + 19)
                dve.sem_inc(freed["D"], 1)
                dve.wait_ge(ring_full, full_count(b, "vcT", 0, last))
                dve.tensor_copy(big["V"][:, bass.ds(b * H, H), NT, :],
                                bank[1][:, 0:DM].rearrange("p (h e) -> p h e", h=H)).then_inc(freed["D"], 1)

            normalise(0, 0)
            dve.wait_ge(ring_full, 2)
            dve.tensor_copy(xnT[0][:, 1, :], bank[1][:, :]).then_inc(freed["D"], 1)
            with dve.Fori(0, B - 1) as b:
                batch(b, False)
            batch(B - 1, True)

        @blk.tensor
        def _(pe):
            def ring_wait(b, name, cc, last):
                u = units(last).index((name, cc))
                if u >= 2:
                    who = owner[units(last)[u - 2][0]]
                    pe.wait_ge(freed[who], freed_count(b, who, u - 1, last))
                else:
                    pe.wait_ge(freed["D"], freed_count(b, "D", 0, last) + u - 1)

            def transpose_xn(cc, f, out):
                for t in range(4):
                    i = pe.transpose(out[:, t * P:(t + 1) * P], xn[cc % 2][:, t, f * P:(f + 1) * P], ident[:, :])
                i.then_inc(ring_full, 1)

            def batch(b, last):
                for cc in range(4):
                    p = cc % 2
                    ahead = not (last and cc == 3)
                    at = units(last).index(("xT1", cc)) + 1 if cc else 0
                    pe.wait_ge(freed["A"], freed_count(b, "A", at, last))
                    pe.wait_ge(freed["D"], freed_count(b, "D", at, last))
                    for m, (n, f) in enumerate((n, f) for n in "qkv" for f in range(2)):
                        if m < 4:
                            pe.wait_ge(rest_ok, b * 18 + (4 * cc + m - 3 if cc else 0) + 1)
                        else:
                            pe.wait_ge(vT_ok, b * 8 + 2 * cc + 1)
                        for k in range(2):
                            i = pe.matmul(bank[2 + m][:, :], W[n][:, k, f * P:(f + 1) * P], xnT[p][:, k, :],
                                          start=(k == 0), stop=(k == 1))
                        i.then_inc(proj, 1)
                    if ahead:
                        pe.wait_ge(xn_ok, b * 4 + cc + 4)
                        for f in range(2):
                            ring_wait(b, f"xT{f}", cc + 1, last)
                            transpose_xn(cc + 1, f, ring_bank(f"xT{f}", cc + 1, last))
                    ring_wait(b, "gr", cc, last)
                    out = ring_bank("gr", cc, last)
                    if cc == 0:
                        pe.wait_ge(diag_in, 16 * 24)
                    pe.wait_ge(first_ok, b * 18 + 4 * cc + 2)
                    for t in range(4):
                        for f in range(2):
                            pe.matmul(out[:, 11 * t:11 * t + 3], qT[:, f, t * P:(t + 1) * P], WG[:, :],
                                      start=(f == 0 and t == 0), stop=(f == 1), skip_group_check=True)
                        for k in range(2):
                            i = pe.matmul(out[:, 11 * t + 3:11 * t + 11], xnT[p][:, k, t * P:(t + 1) * P],
                                          WR[:, k, :], start=False, stop=(k == 1), skip_group_check=True)
                    i.then_inc(ring_full, 1)
                    pe.wait_ge(vT_ok, b * 8 + 2 * cc + 3)
                    for t2 in range(2):
                        ring_wait(b, f"vt{t2}", cc, last)
                        out = ring_bank(f"vt{t2}", cc, last)
                        for t in range(2):
                            for f in range(2):
                                i = pe.transpose(out[:, t * DM + f * P:t * DM + (f + 1) * P],
                                                 vT[:, f, cc * CH + (2 * t2 + t) * P:cc * CH + (2 * t2 + t + 1) * P],
                                                 ident[:, :])
                        i.then_inc(ring_full, 1)
                ring_wait(b, "kcvc", 0, last)
                for w, (src, wt) in enumerate(((kT, WCK), (vT, WCV))):
                    for f in range(2):
                        v = src[:, f, :].rearrange("p (n g) -> p g n", g=G)
                        for g in range(G):
                            i = pe.matmul(bank[0][:, (2 * w + f) * NB:(2 * w + f + 1) * NB], wt[:, g, :], v[:, g, :],
                                          start=(g == 0 and w == 0 and f == 0), stop=(g == G - 1), skip_group_check=True)
                i.then_inc(ring_full, 1)
                ring_wait(b, "vcT", 0, last)
                pe.wait_ge(vcT_ok, b + 1)
                for f in range(2):
                    i = pe.transpose(bank[1][:, f * P:(f + 1) * P], vcT[:, f, :], ident[:, :])
                i.then_inc(ring_full, 1)

            pe.wait_ge(const_in, 16 * 5)
            pe.wait_ge(xn_ok, 3)
            for f in range(2):
                transpose_xn(0, f, bank[f])
            with pe.Fori(0, B - 1) as b:
                batch(b, False)
            batch(B - 1, True)


def phase_r(nc, d, big):
    with ExitStack() as ctx:
        def sb(name, shape, dt=F32):
            return ctx.enter_context(nc.sbuf_tensor(name, shape, dt))

        def sem(name):
            return ctx.enter_context(nc.semaphore(name))

        TT = N // P
        pref = [ctx.enter_context(nc.psum_tensor(f"r_pref{k}", [P, TT, E], F32)) for k in range(2)]
        tot = [ctx.enter_context(nc.psum_tensor(f"r_tot{k}", [P, TT, E], F32)) for k in range(2)]
        bgt = sb("r_bg", [P, 3])
        iota8 = sb("r_iota8", [P, E])
        tri = sb("r_tri", [P, P], BF16)
        ones = sb("r_ones", [P, P], BF16)
        onesf = sb("r_onesf", [P, TT])
        tok2 = sb("r_tok2", [P, TT, 2])
        ga = sb("r_ga", [P, TT, 3])
        gm = sb("r_gm", [P, TT])
        top8 = sb("r_top8", [P, TT, 8])
        idx = sb("r_idx", [P, TT, 8], U32)
        idxf = sb("r_idxf", [P, TT, 2])
        ex = sb("r_ex", [P, TT])
        oh = sb("r_oh", [P, 2, TT, E], BF16)
        incl = sb("r_incl", [P, 2, E, TT])
        rank = sb("r_rank", [P, TT, E])
        pos = sb("r_pos", [P, TT, 2])
        ok = sb("r_ok", [P, TT, 2])
        sc = sb("r_sc", [P, TT, 2])
        zi = sb("r_zi", [P, E * CAP // P], I32)

        const_in = sem("r_const_in")
        seq = sem("r_seq")
        gates_in = sem("r_gates_in")
        gates_exp = sem("r_gates_exp")
        diff_in = sem("r_diff_in")
        diff_exp = sem("r_diff_exp")
        onehot = sem("r_onehot")
        counted = sem("r_counted")
        zi_ok = sem("r_zi_ok")
        tab_zero = sem("r_tab_zero")

        landed = {e: sem(f"r_landed_{e}") for e in "PDT"}
        blk = ctx.enter_context(nc.Block())

        @blk.sync
        def _(sp):
            sp.dma_start(bgt[:, :], d["bg"].partition_broadcast(P)).then_inc(const_in, 16)
            sp.dma_start(iota8[:, :], d["iota8"]).then_inc(const_in, 16)
            sp.dma_start(tri[:, :], d["tri"]).then_inc(const_in, 16)
            sp.dma_start(tok2[:, :, :], d["tok2"]).then_inc(const_in, 16)
            sp.wait_ge(zi_ok, 1)
            sp.dma_start(d["tab_d"][0:E * CAP, :].rearrange("(p c) o -> p (c o)", p=P), zi[:, :]).then_inc(tab_zero, 16)
            sp.wait_ge(tab_zero, 16)

        @blk.tensor
        def _(pe):
            pe.wait_ge(onehot, 3)
            for k in range(2):
                pe.matmul(pref[k][:, :, :], tri[:, :], oh[:, k, :, :], start=True, stop=True)
                i = pe.matmul(tot[k][:, :, :], ones[:, :], oh[:, k, :, :], start=True, stop=True)
            i.then_inc(counted, 1)

        @blk.scalar
        def _(act):
            act.wait_ge(gates_in, 1)
            act.activation(ga[:, :, :], ga[:, :, :], ACT.Exp).then_inc(gates_exp, 1)
            act.wait_ge(diff_in, 1)
            act.activation(ex[:, :], ex[:, :], ACT.Exp).then_inc(diff_exp, 1)

        @blk.vector
        def _(dve):
            n = [0]

            def chain(ins):
                n[0] += 1
                ins.then_inc(seq, 1)
                dve.wait_ge(seq, n[0])

            GL = big["GL"]
            dve.memset(zi[:, :], 0).then_inc(zi_ok, 1)
            dve.memset(ones[:, :], 1.0).then_inc(onehot, 1)
            dve.memset(onesf[:, :], 1.0)
            dve.wait_ge(const_in, 64)
            chain(dve.scalar_tensor_tensor(ga[:, :, :], GL[:, :, 0:3], 1.0 / H,
                                           bgt[:, :].unsqueeze(1).to_broadcast([P, TT, 3]), ALU.mult, ALU.add))
            chain(dve.tensor_reduce(gm[:, :], ga[:, :, :], AX.X, ALU.max))
            dve.tensor_tensor(ga[:, :, :], ga[:, :, :], gm[:, :].unsqueeze(2).to_broadcast([P, TT, 3]),
                              ALU.subtract).then_inc(gates_in, 1)
            for t in range(TT):
                i = dve.max(top8[:, t, :], GL[:, t, 3:11])
            chain(i)
            for t in range(TT):
                i = dve.max_index(idx[:, t, :], top8[:, t, :], GL[:, t, 3:11])
            chain(i)
            chain(dve.tensor_copy(idxf[:, :, :], idx[:, :, 0:2]))
            for k in range(2):
                i = dve.tensor_tensor(oh[:, k, :, :], iota8[:, :].unsqueeze(1).to_broadcast([P, TT, E]),
                                      idxf[:, :, k:k + 1].to_broadcast([P, TT, E]), ALU.is_equal)
                i.then_inc(onehot, 1)
            dve.tensor_tensor(ex[:, :], top8[:, :, 1], top8[:, :, 0], ALU.subtract).then_inc(diff_in, 1)
            dve.wait_ge(gates_exp, 1)
            chain(dve.tensor_reduce(gm[:, :], ga[:, :, :], AX.X, ALU.add))
            chain(dve.reciprocal(gm[:, :], gm[:, :]))
            chain(dve.tensor_tensor(ga[:, :, :], ga[:, :, :], gm[:, :].unsqueeze(2).to_broadcast([P, TT, 3]), ALU.mult))
            chain(dve.memset(ga[0:G, :, :].rearrange("p (b t) g -> p b t g", b=B)[:, :, 0, 0:1], 0.0))
            for b in range(B):
                for j, br in enumerate((1, 0, 2)):
                    i = dve.tensor_copy(big["gates"][:, b * H:(b + 1) * H, :, j],
                                        ga[:, b * NT:(b + 1) * NT, br].unsqueeze(1).to_broadcast([P, H, NT]))
            chain(i)
            dve.wait_ge(diff_exp, 1)
            chain(dve.tensor_scalar(gm[:, :], ex[:, :], 1.0, None, ALU.add))
            chain(dve.reciprocal(big["gk"][:, :, 0], gm[:, :]))
            chain(dve.tensor_tensor(big["gk"][:, :, 1], ex[:, :], big["gk"][:, :, 0], ALU.mult))
            dve.wait_ge(counted, 1)
            for k in range(2):
                for e in range(E):
                    i = dve.tensor_tensor_scan(out=incl[:, k, e, :], data0=onesf[:, :], data1=tot[k][:, :, e],
                                               initial=incl[:, 0, e, TT - 1:TT] if k else 0.0,
                                               op0=ALU.mult, op1=ALU.add)
                chain(i)
            for k in range(2):
                chain(dve.tensor_tensor(rank[:, :, :], incl[:, k, :, :].rearrange("p e t -> p t e"), pref[k][:, :, :], ALU.add))
                chain(dve.tensor_tensor(rank[:, :, :], rank[:, :, :], tot[k][:, :, :], ALU.subtract))
                chain(dve.tensor_tensor(rank[:, :, :], rank[:, :, :], oh[:, k, :, :], ALU.mult))
                chain(dve.tensor_reduce(pos[:, :, k], rank[:, :, :], AX.X, ALU.add))
            chain(dve.tensor_scalar(ok[:, :, :], pos[:, :, :], float(CAP), None, ALU.is_lt))
            chain(dve.tensor_tensor(big["gk"][:, :, :], big["gk"][:, :, :], ok[:, :, :], ALU.mult))
            chain(dve.tensor_scalar(pos[:, :, :], pos[:, :, :], float(CAP - 1), None, ALU.min))
            chain(dve.scalar_tensor_tensor(pos[:, :, :], idxf[:, :, :], float(CAP), pos[:, :, :], ALU.mult, ALU.add))
            chain(dve.tensor_copy(big["slot"][:, :, :], pos[:, :, :]))
            chain(dve.tensor_tensor(sc[:, :, :], pos[:, :, :], tok2[:, :, :], ALU.subtract))
            chain(dve.tensor_tensor(sc[:, :, :], sc[:, :, :], ok[:, :, :], ALU.mult))
            chain(dve.tensor_tensor(sc[:, :, :], sc[:, :, :], tok2[:, :, :], ALU.add))
            dve.tensor_copy(big["scat"][:, :, :], sc[:, :, :])


def phase_b(nc, d, big):
    with ExitStack() as ctx:
        def sb(name, shape, dt=F32):
            return ctx.enter_context(nc.sbuf_tensor(name, shape, dt))

        def sem(name):
            return ctx.enter_context(nc.semaphore(name))

        def two(name, shape, dt=F32):
            return [sb(f"b_{name}{i}", shape, dt) for i in range(2)]

        ring = [ctx.enter_context(nc.psum_tensor(f"b_ring{i}", [P, CH], F32)) for i in range(RING)]
        S = [ctx.enter_context(nc.psum_tensor(f"b_scores{i}", [P, CH], F32)) for i in range(SLOTS)]
        accS = ctx.enter_context(nc.psum_tensor("b_acc_sel", [P, CH], F32))
        accB = ctx.enter_context(nc.psum_tensor("b_acc_rest", [P, CH], F32))

        V, gates = big["V"], big["gates"]
        Q = two("q", [P, T], BF16)
        K = two("k", [P, TK], BF16)
        KW = two("kw", [P, T], BF16)
        VH = two("vh", [P, TP, 32])
        PR = two("pr", [P, 4 * CH])
        scs = two("scs", [P, 4, 4 + NB])
        top8 = two("top8", [P, 4, 8])
        rep = two("rep", [P, 4, 4 + NB])
        selm = two("selm", [P, 4, NB], BF16)
        bm = two("bm", [P, 4, NB])
        junk = sb("b_junk", [P, 4, NB])
        mx = two("mx", [P, 4, 3])
        mr = two("mr", [P, 4, 3])
        mp = two("mp", [P, 4, NM], BF16)
        maskT = two("maskT", [P, CH], BF16)
        accS_s = two("accS_s", [P, CH])
        accB_s = two("accB_s", [P, CH])
        rden = sb("b_rden", [P, 4, 3])
        wgt = sb("b_wgt", [P, 4, 3])
        tmp = two("tmp", [P, 4, 3, D])
        att1 = sb("b_att1", [P, 4, D])
        ident = sb("b_ident", [P, P], BF16)
        expand = sb("b_expand", [P, T], BF16)
        cmp_m = sb("b_cmp_m", [P, 4, 32], BF16)
        cmp_m0 = sb("b_cmp_m0", [P, 4, 32], BF16)
        cmp_mT = sb("b_cmp_mT", [P, T], BF16)
        win_m = sb("b_win_m", [P, 2, LW], BF16)
        win_m0 = sb("b_win_m0", [P, 2, LW], BF16)
        win_mT = sb("b_win_mT", [P, WIN + 3 * LW + P], BF16)
        cau = sb("b_cau", [P, P], BF16)
        cauT = sb("b_cauT", [P, P], BF16)
        first4 = sb("b_first4", [P, 8])
        collect = sb("b_collect", [P, 32])
        pick = sb("b_pick", [P, 64])
        pick0 = sb("b_pick0", [P, 96])
        tokid = sb("b_tokid", [P, N // P], I32)
        si = sb("b_si", [P, 2, 2], I32)
        ti = sb("b_ti", [P, 2], I32)

        assert N // P == 2 * (BH // 2)
        const_in = sem("b_const_in")
        filled = sem("b_filled")
        kq_in = [sem(f"b_kq_in{i}") for i in range(2)]
        vh_ok = sem("b_vh_ok")
        ring_full = sem("b_ring_full")
        freed = {"A": sem("b_freed_act"), "D": sem("b_freed_dve")}
        s_full = sem("b_scores_full")
        exp_ok = sem("b_exp_ok")
        pv_ok = sem("b_pv_ok")
        mc0_ok = sem("b_mc0_ok")
        bias_ok = sem("b_bias_ok")
        top_ok = sem("b_top_ok")
        fill_ok = sem("b_fill_ok")
        rep_ok = sem("b_rep_ok")
        selm_ok = sem("b_selm_ok")
        mx_ok = sem("b_mx_ok")
        mp1_ok = sem("b_mp1_ok")
        mr1_ok = sem("b_mr1_ok")
        mp2_ok = sem("b_mp2_ok")
        mr2_ok = sem("b_mr2_ok")
        mp_ok = sem("b_mp_ok")
        maxrow_full = sem("b_maxrow_full")
        maxrow_ok = sem("b_maxrow_ok")
        accS_ok = sem("b_accS_ok")
        accB_ok = sem("b_accB_ok")
        rden_ok = sem("b_rden_ok")
        wgt_ok = sem("b_wgt_ok")
        tmp_ok = sem("b_tmp_ok")
        att1_ok = sem("b_att1_ok")
        att_ok = sem("b_att_ok")
        si_ok = sem("b_si_ok")
        scat_out = sem("b_scat_out")

        consts = [("ident_b", ident), ("expand", expand), ("cmp_m", cmp_m), ("cmp_m0", cmp_m0), ("cmp_mT", cmp_mT), ("win_m", win_m),
                  ("win_m0", win_m0), ("win_mT", win_mT), ("cau", cau), ("cauT", cauT), ("first4", first4),
                  ("collect", collect), ("pick", pick), ("pick0", pick0), ("tokid", tokid)]

        consts_total = 16 * (len(consts) + 4)

        def body_starts(i):
            return dict(step=i * (2 * NC), unit=i * (2 * UNITS_H), group=i * (2 * GROUPS_H), head=i * 2,
                        ru=i * RU, ra=i * RA, rd=i * RD, i=i)

        landed = {e: sem(f"b_landed_{e}") for e in "PDT"}
        blk = ctx.enter_context(nc.Block())

        @blk.sync
        def _(sp):
            for n, t in consts:
                sp.dma_start(t[:], d[n]).then_inc(const_in, 16)
            for p in range(2):
                sp.dma_start(K[p][QK:ROWS, :], d["k_ones"]).then_inc(const_in, 16)
                sp.dma_start(KW[p][QK:ROWS, :], d["kw_ones"]).then_inc(const_in, 16)

            def load(head, p):
                for r, (a, b) in enumerate(((0, 0), (0, 1), (0, 2), (1, 0), (1, 1), (2, 0))):
                    rows = slice(D * r, D * r + D)
                    sp.dma_start(Q[p][rows, :], d["qp_d"][a, bass.ds(head * D, D), :]).then_inc(kq_in[p], 16)
                    sp.dma_start(K[p][rows, :], d["kp_d"][b, bass.ds(head * D, D), :]).then_inc(kq_in[p], 16)
                    sp.dma_start(KW[p][rows, :], d["kp_d"][b, bass.ds(head * D, D), 0:T]).then_inc(kq_in[p], 16)

            load(0, 0)
            load(1, 1)
            with sp.Fori(0, BH // 2 - 1) as i:
                for p in range(2):
                    sp.wait_ge(pv_ok, i * (2 * GROUPS_H) + GROUPS_H * (p + 1) + 2)
                    load(i * 2 + 2 + p, p)

        LOADS = 18 * 16

        @blk.tensor
        def _(pe):
            def form_ring(kind, r, kk, c, p, mpar, u, before, n, first_load=None):
                out = ring[u % RING]
                if before is not None:
                    who, k = before
                    pe.wait_ge(freed[who], (n["ra"] if who == "A" else n["rd"]) + k)
                q0 = c * CH
                if kind == "scs":
                    if first_load is not None:
                        pe.wait_ge(kq_in[p], first_load)
                    ov = out[:, :].rearrange("p (t n) -> p t n", t=4)
                    pe.matmul(ov[:, :, 32 * c:32 * c + 32], ident[:, :], (cmp_m if c else cmp_m0)[:, :, :], start=True, stop=False,
                              skip_group_check=True)
                    for t in range(4):
                        i = pe.matmul(ov[:, t, 0:32 * (c + 1)], Q[p][0:QK, q0 + t * P:q0 + (t + 1) * P],
                                      K[p][0:QK, T:T + 32 * (c + 1)], start=False, stop=True, skip_group_check=True)
                elif kind == "loc":
                    m = win_m0 if c == 0 and r == 0 else win_m
                    ov = out[:, 0:2 * LW].rearrange("p (t n) -> p t n", t=2)
                    pe.matmul(ov, ident[:, :], m[:, :, :], start=True, stop=False, skip_group_check=True)
                    for t in range(2):
                        tile = 4 * c + 2 * r + t
                        lo = WIN if tile == 0 else 0
                        i = pe.matmul(ov[:, t, lo:LW], Q[p][0:QK, tile * P:(tile + 1) * P],
                                      K[p][0:QK, tile * P - WIN + lo:tile * P + P], start=False, stop=True,
                                      skip_group_check=True)
                elif kind == "S":
                    w = CH if kk < c else P * (r + 1)
                    edge = c == 0 and r == 0
                    i = pe.matmul(out[:, 0:w], Q[p][0:QK, q0 + r * P:q0 + (r + 1) * P],
                                  K[p][0:QK, kk * CH:kk * CH + w], start=True, stop=not edge)
                    if edge:
                        i = pe.matmul(out[:, 0:w], ident[:, :], cau[:, :], start=False, stop=True)
                elif kind == "maskT":
                    nb = 32 * (c + 1)
                    pe.wait_ge(selm_ok, n["next"] + 1)
                    land(pe, landed["T"])
                    ob = out[:, :].bitcast(BF16)
                    for t in range(4):
                        i = pe.transpose(ob[0:nb, t * P:(t + 1) * P], selm[mpar][:, t, 0:nb], ident[:, :])
                else:
                    pe.wait_ge(accS_ok, n["s"] + 2)
                    pe.wait_ge(accB_ok, n["s"] + 2)
                    ov = out[:, :].rearrange("p (t n) -> p t n", t=4)
                    for t in range(4):
                        if c:
                            pe.matmul(ov[:, t, 0:32], accS_s[mpar][:, t * P:(t + 1) * P], collect[:, :],
                                      start=(t == 0), stop=True, skip_group_check=True)
                        else:
                            i = pe.matmul(ov[:, t, 0:96], accB_s[mpar][:, t * P:(t + 1) * P], pick0[:, :],
                                          start=(t == 0), stop=True, skip_group_check=True)
                    for t in range(4 if c else 0):
                        i = pe.matmul(ov[:, t, 32:96], accB_s[mpar][:, t * P:(t + 1) * P], pick[:, :],
                                      start=False, stop=True, skip_group_check=True)
                i.then_inc(ring_full, 1)

            def max_rows(step, par):
                pe.wait_ge(mp_ok, step + 1)
                pe.wait_ge(maxrow_ok, step + 1)
                for t in range(4):
                    i = pe.matmul(accB[QK:ROWS, t * P:(t + 1) * P], mp[par][:, t, :], ident[:, :],
                                  start=True, stop=True, tile_position=(0, QK), skip_group_check=True)
                i.then_inc(maxrow_full, 1)

            def scores(c, u, slot, at_once, p, par, unit):
                pe.wait_ge(exp_ok, unit + (SLOTS if at_once else 1))
                segs, out, q0 = banks_of(c)[u], S[slot], c * CH
                if segs[0][0] == "L":
                    i = pe.matmul(out[:, :], ident[:, :], win_mT[:, 0:CH], start=True, stop=False, skip_group_check=True)
                for si_, (kind, j, q, w, at) in enumerate(segs):
                    qs = Q[p][0:ROWS, q0 + q:q0 + q + w]
                    o = out[:, at:at + w]
                    if kind == "C":
                        pe.matmul(o, K[p][0:ROWS, T:TK], qs, start=True, stop=False, skip_group_check=True)
                        i = pe.matmul(o, ident[:, :], cmp_mT[:, q0:q0 + CH], start=False, stop=True, skip_group_check=True)
                    elif kind == "L":
                        if segs[0][0] != "L":
                            pe.matmul(o, ident[:, :], win_mT[:, CH:CH + P], start=False, stop=False, skip_group_check=True)
                        i = pe.matmul(o, KW[p][0:ROWS, j * P:(j + 1) * P], qs, start=False, stop=True, skip_group_check=True)
                    else:
                        pe.matmul(o, K[p][0:ROWS, j * P:(j + 1) * P], qs, start=(si_ == 0), stop=False, skip_group_check=True)
                        i = pe.matmul(o, expand[:, j * P:(j + 1) * P], maskT[par][:, q:q + w], start=False, stop=True,
                                      skip_group_check=True)
                        if c == 0 and j == 0:
                            i = pe.matmul(out[:, 0:P], ident[:, :], cauT[:, :], start=False, stop=True, skip_group_check=True)
                i.then_inc(s_full, 1)

            def values(c, g, p, unit_end, gpar, started):
                pe.wait_ge(exp_ok, unit_end + SLOTS)
                for pos, segs in enumerate(banks_of(c)[4 * g:4 * g + 4]):
                    for kind, j, q, w, at in segs:
                        pr = PR[gpar][:, pos * CH + at:pos * CH + at + w]
                        if kind == "S":
                            col = 32 * pos if c else 64
                            out = accS[col:col + 32, q:q + w]
                        elif kind == "C":
                            out, col = accB[0:32, q:q + w], 0
                        else:
                            out, col = accB[32:64, q:q + w], 32
                        start = (kind, col) not in started
                        started.add((kind, col))
                        i = pe.matmul(out, VH[p][:, j, :], pr, start=start, stop=False, tile_position=(0, col),
                                      skip_group_check=True)
                i.then_inc(pv_ok, 1)

            def step(n, ls, last):
                c, hp, p, par = chunk_of(ls), ls // NC, ls // NC % 2, ls % 2
                nls = ls + 1
                nxt = None if last else chunk_of(nls)
                s = n["step"] + ls
                u0, g0 = unit_before(ls), group_before(ls)
                started = set()
                for it in step_plan(c, nxt, ls == 0):
                    if it[0] == "ring":
                        _, kind, r, kk = it
                        u, before = rg.next(kind)
                        if kind == "out":
                            form_ring(kind, r, kk, chunk_of(ls - 1), p, (ls - 1) % 2, u, before, dict(n, s=s - 1))
                        else:
                            need = None
                            if kind == "scs" and nls % NC == 0:
                                need = (n["i"] + 1 + nls // (2 * NC)) * LOADS
                            form_ring(kind, r, kk, nxt, nls // NC % 2, nls % 2, u, before, dict(n, next=s + 1), need)
                    elif it[0] == "maxrows":
                        max_rows(s + 1, nls % 2)
                    elif it[0] == "scores":
                        u = it[1]
                        if u == 0:
                            pe.wait_ge(maxrow_ok, s + 2)
                        scores(c, u, *slot_of(ls, u), p, par, n["unit"] + u0 + u)
                    else:
                        g = it[1]
                        if g == 0:
                            if ls % NC == 0:
                                pe.wait_ge(vh_ok, n["head"] + hp + 1)
                            pe.wait_ge(accS_ok, s + 1)
                            pe.wait_ge(accB_ok, s + 1)
                            land(pe, landed["T"])
                        last_u = min(4 * g + 3, units_of(c) - 1)
                        values(c, g, p, n["unit"] + u0 + last_u + 1, (g0 + g) % 2, started)

            pe.wait_ge(const_in, consts_total)
            pe.wait_ge(filled, 1)
            pe.sem_inc(pv_ok, 2)
            rg = Ring()
            n0 = dict(body_starts(0), next=0)
            for kind, r, kk in PRO:
                u, before = rg.next(kind)
                form_ring(kind, r, kk, 0, 0, 0, u, before, n0, LOADS if kind == "scs" else None)
            max_rows(0, 0)
            step(n0, 0, False)
            with pe.Fori(0, BH // 2 - 1) as i:
                rg = ring_at_body()
                for ls in range(1, 2 * NC + 1):
                    step(body_starts(i), ls, False)
            rg = ring_at_body()
            for ls in range(1, 2 * NC):
                step(body_starts(BH // 2 - 1), ls, ls == 2 * NC - 1)
            u, before = rg.next("out")
            form_ring("out", 0, 0, chunk_of(2 * NC - 1), 1, 1, u, before, dict(body_starts(BH // 2 - 1), s=BH * NC - 1))

        @blk.scalar
        def _(act):
            def ring_unit(kind, c, p, par, u, n, step):
                act.wait_ge(ring_full, n["ru"] + u + 1)
                out = ring[u % RING]
                if kind == "scs":
                    act.wait_ge(rep_ok, step + 1)
                    act.copy(scs[par][:, :, 4:4 + 32 * (c + 1)],
                             out[:, :].rearrange("p (t n) -> p t n", t=4)[:, :, 0:32 * (c + 1)]).then_inc(freed["A"], 1)
                else:
                    nb = 32 * (c + 1)
                    act.copy(maskT[par][0:nb, :], out[0:nb, :].bitcast(BF16)[:, 0:CH]).then_inc(freed["A"], 1)

            def max_rows(c, p, step):
                act.wait_ge(maxrow_full, step + 1)
                act.copy(Q[p][QK:ROWS, c * CH:(c + 1) * CH], accB[QK:ROWS, :]).then_inc(maxrow_ok, 1)

            def step(n, ls, last):
                c, par, nls = chunk_of(ls), ls % 2, ls + 1
                nxt = None if last else chunk_of(nls)
                np_ = nls // NC % 2
                s = n["step"] + ls
                u0, g0 = unit_before(ls), group_before(ls)
                for it in step_plan(c, nxt, ls == 0):
                    if it[0] == "ring":
                        u, _ = rg.next(it[1])
                        if it[1] in ("scs", "maskT"):
                            ring_unit(it[1], nxt, np_, nls % 2, u, n, s + 1)
                    elif it[0] == "maxrows":
                        max_rows(nxt, np_, s + 1)
                    elif it[0] == "scores":
                        u = it[1]
                        g = u // 4
                        w = max(seg[4] + seg[3] for seg in banks_of(c)[u])
                        act.wait_ge(s_full, n["unit"] + u0 + u + 1)
                        if u % 4 == 0:
                            act.wait_ge(pv_ok, n["group"] + g0 + g + 1)
                        at = (u % 4) * CH
                        act.activation(PR[(g0 + g) % 2][:, at:at + w], S[slot_of(ls, u)[0]][:, 0:w], ACT.Exp).then_inc(exp_ok, 1)
                act.wait_ge(pv_ok, n["group"] + g0 + c + 2 + 2)
                act.copy(accB_s[par][0:64, :], accB[0:64, :]).then_inc(accB_ok, 1)
                if c:
                    act.copy(accS_s[par][:, :], accS[:, :]).then_inc(accS_ok, 1)
                else:
                    act.copy(accB_s[par][64:96, :], accS[64:96, :]).then_inc(accS_ok, 1)

            act.sem_inc(exp_ok, SLOTS)
            act.sem_inc(accB_ok, 1)
            act.sem_inc(maxrow_ok, 1)
            rg = Ring()
            n0 = body_starts(0)
            for kind, r, kk in PRO:
                u, _ = rg.next(kind)
                if kind in ("scs", "maskT"):
                    ring_unit(kind, 0, 0, 0, u, n0, 0)
            max_rows(0, 0, 0)
            step(n0, 0, False)
            with act.Fori(0, BH // 2 - 1) as i:
                rg = ring_at_body()
                for ls in range(1, 2 * NC + 1):
                    step(body_starts(i), ls, False)
            rg = ring_at_body()
            for ls in range(1, 2 * NC):
                step(body_starts(BH // 2 - 1), ls, ls == 2 * NC - 1)

        @blk.vector
        def _(dve):
            def reduce_unit(kind, r, kk, c, par, u, n):
                dve.wait_ge(ring_full, n["ru"] + u + 1)
                out = ring[u % RING]
                if kind == "loc":
                    dve.tensor_reduce(mx[par][:, 2 * r:2 * r + 2, 2], out[:, 0:2 * LW].rearrange("p (t n) -> p t n", t=2),
                                      AX.X, ALU.max).then_inc(freed["D"], 1)
                else:
                    w = CH if kk < c else P * (r + 1)
                    dve.tensor_reduce(bm[par][:, r, 32 * kk:32 * kk + w // G],
                                      out[:, 0:w].rearrange("p (n g) -> p n g", g=G), AX.X, ALU.max).then_inc(freed["D"], 1)

            def choose(c, par, step, head, scs_count):
                nb = 32 * (c + 1)
                dve.wait_ge(freed["A"], scs_count)
                if c == 0:
                    dve.tensor_reduce(mx[par][:, 0, 1:2], scs[par][:, 0, 4:12], AX.X, ALU.max)
                    dve.tensor_tensor(scs[par][:, 0, 4:12], scs[par][:, 0, 4:12], first4[:, :], ALU.add).then_inc(bias_ok, 1)
                    dve.wait_ge(bias_ok, head + 1)
                land(dve, landed["D"])
                for t in range(4):
                    i = dve.max(top8[par][:, t, :], scs[par][:, t, 4:4 + nb])
                i.then_inc(top_ok, 1)

            def mark(c, par, step):
                nb = 32 * (c + 1)
                dve.wait_ge(top_ok, step + 1)
                lo = 1 if c == 0 else 0
                dve.tensor_copy(mx[par][:, lo:4, 1], top8[par][:, lo:4, 0])
                dve.memset(top8[par][:, :, 4:8], FAR).then_inc(fill_ok, 1)
                dve.wait_ge(fill_ok, step + 1)
                land(dve, landed["D"])
                for t in range(4):
                    i = dve.match_replace(rep[par][:, t, 0:4 + nb], top8[par][:, t, :], scs[par][:, t, 0:4 + nb], FOUND)
                i.then_inc(rep_ok, 1)

            def maxima(c, par, step, reduced):
                dve.wait_ge(selm_ok, step + 1)
                dve.wait_ge(freed["D"], reduced)
                land(dve, landed["D"])
                for t in range(4):
                    nb = 8 * (4 * c + t + 1)
                    i = dve.tensor_tensor_reduce(out=junk[:, t, 0:nb], in0=bm[par][:, t, 0:nb], in1=selm[par][:, t, 0:nb],
                                                 scale=1.0, scalar=FAR, op0=ALU.add, op1=ALU.max,
                                                 accum_out=mx[par][:, t, 0:1])
                i.then_inc(mx_ok, 1)
                parts = mp[par][:, :, :].rearrange("p t (b i) -> p t b i", i=3)
                dve.wait_ge(mx_ok, step + 1)
                dve.tensor_scalar(parts[:, :, :, 0], mx[par][:, :, :], -1.0, None, ALU.mult).then_inc(mp1_ok, 1)
                dve.wait_ge(mp1_ok, step + 1)
                dve.scalar_tensor_tensor(mr[par][:, :, :], mx[par][:, :, :], -1.0, parts[:, :, :, 0], ALU.mult,
                                         ALU.subtract).then_inc(mr1_ok, 1)
                dve.wait_ge(mr1_ok, step + 1)
                dve.tensor_copy(parts[:, :, :, 1], mr[par][:, :, :]).then_inc(mp2_ok, 1)
                dve.wait_ge(mp2_ok, step + 1)
                dve.tensor_tensor(parts[:, :, :, 2], mr[par][:, :, :], parts[:, :, :, 1], ALU.subtract).then_inc(mp_ok, 1)

            def results(c, hp, par, u, n, s):
                dve.wait_ge(ring_full, n["ru"] + u + 1)
                ov = ring[u % RING][:, :].rearrange("p (t n) -> p t n", t=4)[:, :, 0:96].rearrange("p t (b e) -> p t b e", b=3)
                dve.reciprocal(rden[:, :, :], ov[:, :, :, D]).then_inc(rden_ok, 1)
                dve.wait_ge(rden_ok, s + 1)
                dve.tensor_tensor(wgt[:, :, :].unsqueeze(1), rden[:, :, :].unsqueeze(1),
                                  gates[:, bass.ds(n["head"] + hp, 1), 4 * c:4 * c + 4, :], ALU.mult).then_inc(wgt_ok, 1)
                dve.wait_ge(wgt_ok, s + 1)
                dve.wait_ge(att_ok, s + 1)
                dve.tensor_tensor(tmp[par][:, :, :, :], ov[:, :, :, 0:D],
                                  wgt[:, :, :].unsqueeze(3).to_broadcast([P, 4, 3, D]), ALU.mult).then_inc(freed["D"], 1)

            def step(n, ls, last):
                c, par, nls = chunk_of(ls), ls % 2, ls + 1
                nxt = None if last else chunk_of(nls)
                s = n["step"] + ls
                scs_count, seen, formed = None, 0, None
                g0 = group_before(ls)
                for it in step_plan(c, nxt, ls == 0):
                    if it[0] == "ring":
                        _, kind, r, kk = it
                        u, _ = rg.next(kind)
                        if kind == "scs":
                            scs_count = n["ra"] + rg.owners[-1][1]
                        elif kind in ("loc", "S"):
                            reduce_unit(kind, r, kk, nxt, nls % 2, u, n)
                        elif kind == "out":
                            formed = u
                        seen += 1
                        if nxt is not None and seen == AT_TOP:
                            choose(nxt, nls % 2, s + 1, n["head"] + nls // NC, scs_count)
                        if nxt is not None and seen == AT_FOUND:
                            mark(nxt, nls % 2, s + 1)
                    elif it[0] == "maxrows":
                        maxima(nxt, nls % 2, s + 1, n["rd"] + rg.freed["D"] - (formed is not None))
                if formed is not None:
                    results(chunk_of(ls - 1), (ls - 1) // NC, (ls - 1) % 2, formed, n, s - 1)

            for p in range(2):
                dve.memset(VH[p][:, :, D + 1:32], 0.0)
                dve.memset(VH[p][:, :, D:D + 1], 1.0)
                dve.memset(scs[p][:, :, 0:4], FAR)
                dve.memset(accS_s[p][:, :], 0.0)
                dve.memset(accB_s[p][:, :], 0.0)
                i = dve.memset(maskT[p][:, :], 0.0)
            i.then_inc(filled, 1)
            dve.sem_inc(rep_ok, 2)
            dve.sem_inc(accS_ok, 1)
            dve.wait_ge(const_in, consts_total)
            rg = Ring()
            n0 = body_starts(0)
            for kind, r, kk in PRO:
                u, _ = rg.next(kind)
                if kind == "scs":
                    scs_count = rg.owners[-1][1]
                elif kind in ("loc", "S"):
                    reduce_unit(kind, r, kk, 0, 0, u, n0)
            choose(0, 0, 0, 0, scs_count)
            mark(0, 0, 0)
            maxima(0, 0, 0, rg.freed["D"])
            step(n0, 0, False)
            with dve.Fori(0, BH // 2 - 1) as i:
                rg = ring_at_body()
                for ls in range(1, 2 * NC + 1):
                    step(body_starts(i), ls, False)
            rg = ring_at_body()
            for ls in range(1, 2 * NC):
                step(body_starts(BH // 2 - 1), ls, ls == 2 * NC - 1)
            u, _ = rg.next("out")
            results(chunk_of(2 * NC - 1), 1, 1, u, body_starts(BH // 2 - 1), BH * NC - 1)

        @blk.gpsimd
        def _(pool):
            def values_of(head, p):
                land(pool, landed["P"])
                pool.tensor_copy(VH[p][:, :, 0:D].unsqueeze(1), V[:, bass.ds(head, 1), :, :]).then_inc(vh_ok, 1)

            def masks(c, par, step):
                nb = 32 * (c + 1)
                pool.wait_ge(rep_ok, step + 3)
                land(pool, landed["P"])
                pool.tensor_scalar(selm[par][:, :, 0:nb], rep[par][:, :, 4:4 + nb], 1.0e38, NEG, ALU.is_lt,
                                   ALU.mult).then_inc(selm_ok, 1)

            def sum_up(ls, n):
                c, hp, par, s = chunk_of(ls), ls // NC, ls % 2, n["step"] + ls
                pool.wait_ge(freed["D"], n["rd"] + rg.freed["D"])
                pool.wait_ge(att_ok, s + 2)
                pool.tensor_tensor(att1[:, :, :], tmp[par][:, :, 0, :], tmp[par][:, :, 1, :], ALU.add).then_inc(att1_ok, 1)
                pool.wait_ge(att1_ok, s + 1)
                pool.wait_ge(vh_ok, n["head"] + hp + 1)
                pool.tensor_tensor(V[:, bass.ds(n["head"] + hp, 1), 4 * c:4 * c + 4, :], att1[:, :, :].unsqueeze(1),
                                   tmp[par][:, :, 2, :].unsqueeze(1), ALU.add).then_inc(att_ok, 1)

            def rows_of(turn):
                pool.tensor_copy(si[:, :, :], big["scat"][:, bass.ds(turn * 2, 2), :]).then_inc(si_ok, 1)
                pool.tensor_copy(ti[:, :], tokid[:, bass.ds(turn * 2, 2)]).then_inc(si_ok, 1)

            def scatter(turn, t):
                if t == 0:
                    pool.wait_ge(si_ok, turn * 2 + 2)
                    land(pool, landed["P"])
                for k in range(2):
                    pool.indirect_dma_start(
                        out=d["tab_d"], out_offset=bass.IndirectOffsetOnAxis(ap=si[:, t, k:k + 1], axis=0),
                        in_=ti[:, t:t + 1], in_offset=None).then_inc(scat_out, 16)

            def step(n, ls, last):
                c, hp = chunk_of(ls), ls // NC
                nxt = None if last else chunk_of(ls + 1)
                s = n["step"] + ls
                for it in step_plan(c, nxt, ls == 0):
                    if it[0] != "ring":
                        continue
                    rg.next(it[1])
                    if it[1] == "maskT":
                        masks(nxt, (ls + 1) % 2, s + 1)
                    elif it[1] == "out":
                        sum_up(ls - 1, n)
                if ls % NC == NC - 1 and not n.get("tail"):
                    pool.wait_ge(pv_ok, n["group"] + GROUPS_H * (hp + 1) + 2)
                    values_of(n["head"] + hp + 2, hp % 2)

            pool.wait_ge(filled, 1)
            pool.sem_inc(att_ok, 2)
            values_of(0, 0)
            values_of(1, 1)
            rg = Ring()
            for kind, _, _ in PRO:
                rg.next(kind)
            masks(0, 0, 0)
            pool.wait_ge(const_in, consts_total)
            rows_of(0)
            scatter(0, 0)
            scatter(0, 1)
            step(body_starts(0), 0, False)
            with pool.Fori(0, BH // 2 - 1) as i:
                rg = ring_at_body()
                for ls in range(1, 2 * NC + 1):
                    step(body_starts(i), ls, False)
                    if ls == 1:
                        pool.wait_ge(scat_out, i * 64 + 64)
                        land(pool, landed["P"])
                        rows_of(i + 1)
                    elif ls in (4, 6):
                        scatter(i + 1, ls // 2 - 2)
            rg = ring_at_body()
            for ls in range(1, 2 * NC):
                step(dict(body_starts(BH // 2 - 1), tail=True), ls, ls == 2 * NC - 1)
            rg.next("out")
            sum_up(2 * NC - 1, body_starts(BH // 2 - 1))
            pool.wait_ge(scat_out, 64 * (BH // 2))


def phase_c(nc, d):
    with ExitStack() as ctx:
        def two(name, shape, dt=F32):
            return [ctx.enter_context(nc.sbuf_tensor(f"c_{name}{i}", shape, dt)) for i in range(2)]

        def sem(name):
            return ctx.enter_context(nc.semaphore(name))

        bank = [ctx.enter_context(nc.psum_tensor(f"c_bank{i}", [P, CH], F32)) for i in range(8)]
        ident = ctx.enter_context(nc.sbuf_tensor("c_ident", [P, P], F32))
        w1 = two("w1", [P, 2, HID])
        w2 = two("w2", [P, HID // P, DM])
        b1 = two("b1", [P, HID // P])
        b2 = two("b2", [P, DM])
        ids = two("ids", [P, CAP // P], I32)
        xg = two("xg", [P, 4, DM])
        xT = two("xT", [P, 2, CH])
        hT = two("hT", [P, HID // P, CH])
        ys = two("ys", [P, 4, DM])
        NM8 = HID // P

        ident_in = sem("c_ident_in")
        w_in = [sem(f"c_w_in{i}") for i in range(2)]
        x_in = [sem(f"c_x_in{i}") for i in range(2)]
        turned = sem("c_turned")
        xT0_ok, xT1_ok = sem("c_xT0_ok"), sem("c_xT1_ok")
        h_full, h_ok = sem("c_h_full"), sem("c_h_ok")
        y_full, y_ok = sem("c_y_full"), sem("c_y_ok")
        y_out = [sem(f"c_y_out{i}") for i in range(2)]

        def load_next(sp, load, i):
            load(((i * 2) + 2) % E, 0)

        landed = {e: sem(f"c_landed_{e}") for e in "PDT"}
        blk = ctx.enter_context(nc.Block())

        @blk.sync
        def _(sp):
            sp.dma_start(ident[:, :], d["ident_f"]).then_inc(ident_in, 16)

            def load(e, p):
                sp.dma_start(w1[p][:, :, :].unsqueeze(1), d["w1"][bass.ds(e, 1)].rearrange("e (k p) n -> p e k n", p=P)).then_inc(w_in[p], 16)
                sp.dma_start(w2[p][:, :, :].unsqueeze(1), d["w2"][bass.ds(e, 1)].rearrange("e (k p) n -> p e k n", p=P)).then_inc(w_in[p], 16)
                sp.dma_start(b1[p][:, :].unsqueeze(1), d["b1"][bass.ds(e, 1)].rearrange("e (k p) -> p e k", p=P),
                             allow_slow_non_contiguous=True).then_inc(w_in[p], 16)
                sp.dma_start(b2[p][:, :], d["b2"][bass.ds(e, 1)].to_broadcast([P, DM])).then_inc(w_in[p], 16)
                sp.dma_start(ids[p][:, :], d["tab_d"][bass.ds(e * CAP, CAP), :].rearrange("(p t) o -> p (t o)", p=P)).then_inc(w_in[p], 16)

            load(0, 0)
            with sp.Fori(0, E // 2) as i:
                for p in range(2):
                    for cc in range(4):
                        k = 4 * p + cc
                        if cc == 1:
                            if p == 0:
                                load(i * 2 + 1, 1)
                            else:
                                load_next(sp, load, i)
                        sp.wait_ge(y_ok, i * 16 + 2 * k + 4)
                        sp.dma_start(d["y_d"][bass.ds((i * 2 + p) * CAP, CAP), :].rearrange(
                            "(p t) m -> p t m", p=P)[:, 4 * cc:4 * cc + 4, :],
                                     ys[k % 2][:, :, :]).then_inc(y_out[k % 2], 16)
            for p in range(2):
                sp.wait_ge(y_out[p], 16 + 16 * E * 2)

        @blk.gpsimd
        def _(pool):
            def gather(i, p, cc):
                k = 4 * p + cc
                pool.wait_ge(turned, i * 16 + 2 * k + 1)
                land(pool, landed["P"])
                for t in range(4):
                    pool.indirect_dma_start(
                        out=xg[k % 2][:, t, :], out_offset=None, in_=d["xn_d"].rearrange("b t m -> (b t) m"),
                        in_offset=bass.IndirectOffsetOnAxis(ap=ids[p][:, 4 * cc + t:4 * cc + t + 1], axis=0)
                    ).then_inc(x_in[k % 2], 16)

            pool.sem_inc(y_out[0], 16)
            pool.sem_inc(y_out[1], 16)
            with pool.Fori(0, E // 2) as i:
                for p in range(2):
                    pool.wait_ge(w_in[p], i * 80 + 80)
                    for cc in range(4):
                        gather(i, p, cc)
            pool.wait_ge(w_in[0], E // 2 * 80 + 80)
            gather(E // 2, 0, 0)

        @blk.tensor
        def _(pe):
            def turn(i, k):
                pe.wait_ge(x_in[k % 2], i * 256 + 64 * (k // 2) + 64)
                for f in range(2):
                    for t in range(4):
                        m = pe.transpose(bank[f][:, t * P:(t + 1) * P], xg[k % 2][:, t, f * P:(f + 1) * P], ident[:, :])
                    m.then_inc(turned, 1)

            pe.wait_ge(ident_in, 16)
            pe.sem_inc(turned, 3)
            turn(0, 0)
            with pe.Fori(0, E // 2) as i:
                for p in range(2):
                    pe.wait_ge(w_in[p], i * 80 + 80)
                    for cc in range(4):
                        k = 4 * p + cc
                        pe.wait_ge(xT0_ok, i * 8 + k + 2)
                        pe.wait_ge(xT1_ok, i * 8 + k + 2)
                        for j in range(NM8):
                            pe.wait_ge(h_ok, i * 64 + 8 * k + j + 1)
                            for f in range(2):
                                m = pe.matmul(bank[2 + j % 4][:, :], w1[p][:, f, j * P:(j + 1) * P], xT[k % 2][:, f, :],
                                              start=(f == 0), stop=(f == 1))
                            m.then_inc(h_full, 1)
                        turn(i, k + 1)
                        for t2 in range(2):
                            pe.wait_ge(y_ok, i * 16 + 2 * k + t2 + 1)
                            if t2 == 0:
                                pe.wait_ge(h_ok, i * 64 + 8 * k + 8 + 4)
                            for t in range(2):
                                for j in range(NM8):
                                    m = pe.matmul(bank[6 + t2][:, t * DM:(t + 1) * DM],
                                                  hT[k % 2][:, j, (2 * t2 + t) * P:(2 * t2 + t + 1) * P], w2[p][:, j, :],
                                                  start=(j == 0), stop=(j == NM8 - 1), skip_group_check=True)
                            m.then_inc(y_full, 1)

        @blk.scalar
        def _(act):
            def copy_xT(i, k):
                act.wait_ge(turned, i * 16 + 2 * k + 4)
                act.copy(xT[k % 2][:, 0, :], bank[0][:, :]).then_inc(xT0_ok, 1)

            act.sem_inc(h_ok, 4)
            act.sem_inc(xT0_ok, 1)
            copy_xT(0, 0)
            with act.Fori(0, E // 2) as i:
                for p in range(2):
                    for cc in range(4):
                        k = 4 * p + cc
                        act.wait_ge(w_in[p], i * 80 + 80)
                        for j in range(NM8):
                            act.wait_ge(h_full, i * 64 + 8 * k + j + 1)
                            act.activation(hT[k % 2][:, j, :], bank[2 + j % 4][:, :], ACT.Relu,
                                           bias=b1[p][:, j:j + 1]).then_inc(h_ok, 1)
                        copy_xT(i, k + 1)

        @blk.vector
        def _(dve):
            def copy_xT(i, k):
                dve.wait_ge(turned, i * 16 + 2 * k + 5)
                dve.tensor_copy(xT[k % 2][:, 1, :], bank[1][:, :]).then_inc(xT1_ok, 1)

            dve.sem_inc(xT1_ok, 1)
            dve.sem_inc(y_ok, 2)
            copy_xT(0, 0)
            with dve.Fori(0, E // 2) as i:
                for p in range(2):
                    for cc in range(4):
                        k = 4 * p + cc
                        copy_xT(i, k + 1)
                        dve.wait_ge(w_in[p], i * 80 + 80)
                        for t2 in range(2):
                            dve.wait_ge(y_full, i * 16 + 2 * k + t2 + 1)
                            dve.wait_ge(y_out[k % 2], i * 64 + 16 * (k // 2) + 16)
                            dve.tensor_tensor(ys[k % 2][:, 2 * t2:2 * t2 + 2, :],
                                              bank[6 + t2][:, :].rearrange("p (t m) -> p t m", t=2),
                                              b2[p][:, :].unsqueeze(1).to_broadcast([P, 2, DM]), ALU.add).then_inc(y_ok, 1)


def phase_d(nc, d, big):
    with ExitStack() as ctx:
        def two(name, shape, dt=F32):
            return [ctx.enter_context(nc.sbuf_tensor(f"d_{name}{i}", shape, dt)) for i in range(2)]

        def sem(name):
            return ctx.enter_context(nc.semaphore(name))

        bank = [ctx.enter_context(nc.psum_tensor(f"d_bank{i}", [P, CH], F32)) for i in range(4)]
        ident = ctx.enter_context(nc.sbuf_tensor("d_ident", [P, P], F32))
        Wo = ctx.enter_context(nc.sbuf_tensor("d_Wo", [P, 2, DM], F32))
        xs = two("xs", [P, 4, DM])
        y = [two(f"y{k}", [P, 4, DM]) for k in range(2)]
        att = two("att", [P, 4, H, D])
        attT = two("attT", [P, 2, CH])
        si = two("si", [P, 4, 2], I32)
        gs = two("gs", [P, 4, 2])
        res = two("res", [P, 4, DM])

        const_in = sem("d_const_in")
        x_in = [sem(f"d_x_in{i}") for i in range(2)]
        y_in = [sem(f"d_y_in{i}") for i in range(2)]
        att_ok, si_ok = sem("d_att_ok"), sem("d_si_ok")
        turned, aT0_ok, aT1_ok = sem("d_turned"), sem("d_aT0_ok"), sem("d_aT1_ok")
        o_full, o_ok = sem("d_o_full"), sem("d_o_ok")
        r1_ok, r2_ok = sem("d_r1_ok"), sem("d_r2_ok")
        out_done = [sem(f"d_out_done{i}") for i in range(2)]

        def store(sp, b, cc):
            sp.wait_ge(r2_ok, b * 4 + cc + 3)
            sp.dma_start(d["out"][bass.ds(b, 1), cc * CH:(cc + 1) * CH, :].rearrange("o (t p) m -> p (o t) m", p=P),
                         res[cc % 2][:, :, :]).then_inc(out_done[cc % 2], 16)

        landed = {e: sem(f"d_landed_{e}") for e in "PDT"}
        blk = ctx.enter_context(nc.Block())

        @blk.sync
        def _(sp):
            sp.dma_start(ident[:, :], d["ident_f"]).then_inc(const_in, 16)
            sp.dma_start(Wo[:, :, :], d["Wo"].rearrange("(k p) n -> p k n", p=P)).then_inc(const_in, 16)
            sp.sem_inc(out_done[0], 16)
            sp.sem_inc(out_done[1], 16)
            with sp.Fori(0, B) as b:
                for cc in range(4):
                    p = cc % 2
                    sp.wait_ge(r2_ok, b * 4 + cc + 1)
                    sp.dma_start(xs[p][:, :, :], d["x"][bass.ds(b, 1), cc * CH:(cc + 1) * CH, :].rearrange(
                        "o (t p) m -> p (o t) m", p=P)).then_inc(x_in[p], 16)
                    if cc:
                        store(sp, b, cc - 1)
                store(sp, b, 3)
            for p in range(2):
                sp.wait_ge(out_done[p], 16 + 16 * B * 2)

        @blk.gpsimd
        def _(pool):
            with pool.Fori(0, B) as b:
                for cc in range(4):
                    p = cc % 2
                    pool.wait_ge(r2_ok, b * 4 + cc + 1)
                    land(pool, landed["P"])
                    pool.tensor_copy(si[p][:, :, :], big["slot"][:, bass.ds(b * NT + 4 * cc, 4), :]).then_inc(si_ok, 1)
                    pool.tensor_copy(gs[p][:, :, :], big["gk"][:, bass.ds(b * NT + 4 * cc, 4), :]).then_inc(si_ok, 1)
                    pool.wait_ge(si_ok, b * 8 + 2 * cc + 2)
                    land(pool, landed["P"])
                    for t in range(4):
                        for k in range(2):
                            pool.indirect_dma_start(out=y[k][p][:, t, :], out_offset=None, in_=d["y_d"],
                                                    in_offset=bass.IndirectOffsetOnAxis(ap=si[p][:, t, k:k + 1], axis=0)
                                                    ).then_inc(y_in[p], 16)

        @blk.tensor
        def _(pe):
            pe.wait_ge(const_in, 32)
            pe.sem_inc(turned, 1)
            with pe.Fori(0, B) as b:
                for cc in range(4):
                    p = cc % 2
                    pe.wait_ge(att_ok, b * 4 + cc + 1)
                    pe.wait_ge(aT0_ok, b * 4 + cc + 1)
                    pe.wait_ge(aT1_ok, b * 4 + cc + 1)
                    for f in range(2):
                        for t in range(4):
                            m = pe.transpose(bank[f][:, t * P:(t + 1) * P],
                                             att[p][:, t, 8 * f:8 * f + 8, :].rearrange("p h e -> p (h e)"), ident[:, :])
                        m.then_inc(turned, 1)
                    pe.wait_ge(aT0_ok, b * 4 + cc + 2)
                    pe.wait_ge(aT1_ok, b * 4 + cc + 2)
                    pe.wait_ge(o_ok, b * 8 + 2 * cc + 1)
                    for t2 in range(2):
                        for t in range(2):
                            for f in range(2):
                                m = pe.matmul(bank[2 + t2][:, t * DM:(t + 1) * DM],
                                              attT[p][:, f, (2 * t2 + t) * P:(2 * t2 + t + 1) * P], Wo[:, f, :],
                                              start=(f == 0), stop=(f == 1), skip_group_check=True)
                        m.then_inc(o_full, 1)

        @blk.scalar
        def _(act):
            act.sem_inc(aT0_ok, 1)
            act.sem_inc(aT1_ok, 1)
            with act.Fori(0, B) as b:
                for cc in range(4):
                    act.wait_ge(turned, b * 8 + 2 * cc + 1)
                    act.copy(att[cc % 2][:, :, :, :], big["V"][:, bass.ds(b * H, H), 4 * cc:4 * cc + 4, :].rearrange(
                        "p h t e -> p t h e")).then_inc(att_ok, 1)
                    act.wait_ge(turned, b * 8 + 2 * cc + 2)
                    act.copy(attT[cc % 2][:, 0, :], bank[0][:, :]).then_inc(aT0_ok, 1)
                    act.wait_ge(turned, b * 8 + 2 * cc + 3)
                    act.copy(attT[cc % 2][:, 1, :], bank[1][:, :]).then_inc(aT1_ok, 1)

        @blk.vector
        def _(dve):
            dve.sem_inc(r2_ok, 2)
            dve.sem_inc(o_ok, 1)
            with dve.Fori(0, B) as b:
                for cc in range(4):
                    p = cc % 2
                    dve.wait_ge(x_in[p], b * 32 + 16 * (cc // 2) + 16)
                    dve.wait_ge(out_done[p], b * 32 + 16 * (cc // 2) + 16)
                    for t2 in range(2):
                        dve.wait_ge(o_full, b * 8 + 2 * cc + t2 + 1)
                        dve.tensor_tensor(res[p][:, 2 * t2:2 * t2 + 2, :], bank[2 + t2][:, :].rearrange("p (t m) -> p t m", t=2),
                                          xs[p][:, 2 * t2:2 * t2 + 2, :], ALU.add).then_inc(o_ok, 1)
                    dve.wait_ge(o_ok, b * 8 + 2 * cc + 3)
                    dve.wait_ge(y_in[p], b * 256 + 128 * (cc // 2) + 128)
                    for t in range(4):
                        m = dve.scalar_tensor_tensor(res[p][:, t, :], y[0][p][:, t, :], gs[p][:, t, 0:1], res[p][:, t, :],
                                                     ALU.mult, ALU.add)
                    m.then_inc(r1_ok, 1)
                    dve.wait_ge(r1_ok, b * 4 + cc + 1)
                    for t in range(4):
                        m = dve.scalar_tensor_tensor(res[p][:, t, :], y[1][p][:, t, :], gs[p][:, t, 1:2], res[p][:, t, :],
                                                     ALU.mult, ALU.add)
                    m.then_inc(r2_ok, 1)


def build(nc, d):
    TT = N // P
    with ExitStack() as ctx:
        def sb(name, shape, dt=F32):
            return ctx.enter_context(nc.sbuf_tensor(name, shape, dt))

        big = {
            "V": sb("V", [P, BH, TP, D]),
            "gates": sb("gates", [P, BH, NT, 3]),
            "GL": sb("GL", [P, TT, 3 + E]),
            "gk": sb("gk", [P, TT, 2]),
            "slot": sb("slot", [P, TT, 2], I32),
            "scat": sb("scat", [P, TT, 2], I32),
        }
        phase_a(nc, d, big)
        phase_r(nc, d, big)
        phase_b(nc, d, big)
        phase_c(nc, d)
        phase_d(nc, d, big)


def constants():
    import numpy as np

    def bf(a):
        return (np.ascontiguousarray(a, dtype=np.float32).view(np.uint32) >> 16).astype(np.uint16)

    p, q = np.arange(P)[:, None], np.arange(P)[None, :]

    def mask(bad):
        return bf(np.where(bad, NEG, 0.0))

    t, n = np.arange(T), np.arange(NB)
    cmp_m = np.stack([mask(P * r + p < G * (np.arange(32)[None, :] + 1)) for r in range(4)], 1)
    cmp_m0 = np.stack([mask(np.maximum(P * r + p, G) < G * (np.arange(32)[None, :] + 1)) for r in range(4)], 1)
    y = np.arange(LW)[None, :]
    win = mask((y < p) | (y > p + WIN))
    win0 = mask((y < p) | (y > p + WIN) | (y < WIN))
    winT = mask((y < p) | (y > p + WIN))
    before = mask((np.arange(WIN)[None, :] + P - p) > WIN)
    sel = np.zeros((P, 32), np.float32)
    for g in range(4):
        sel[32 * g + np.arange(32), np.arange(32)] = 1.0
    k_ones = np.zeros((NM, TK), np.float32)
    k_ones[0:3, :T] = 1.0
    k_ones[3:6, T:] = 1.0
    kw_ones = np.zeros((NM, T), np.float32)
    kw_ones[6:9] = 1.0
    tile = np.arange(N // P)
    return {
        "ident_f": np.eye(P, dtype=np.float32),
        "ident_b": bf(np.eye(P)),
        "tri": bf(p < q),
        "iota8": np.tile(np.arange(E, dtype=np.float32), (P, 1)),
        "tok2": (E * CAP + 2.0 * (tile[None, :, None] * P + p[:, :, None]) + np.arange(2)[None, None, :]).astype(np.float32),
        "tokid": (tile[None, :] * P + p).astype(np.int32),
        "expand": bf(t[None, :] // G == n[:, None]),
        "cmp_m": cmp_m,
        "cmp_m0": cmp_m0,
        "cmp_mT": mask(np.maximum(t, G)[None, :] < G * (n[:, None] + 1)),
        "win_m": np.stack([win, win], 1),
        "win_m0": np.stack([win0, win], 1),
        "win_mT": np.concatenate([before, winT, winT, winT, winT[:, :P]], 1),
        "cau": mask(q > p),
        "cauT": mask(p > q),
        "first4": np.where((p < 64) & (np.arange(8)[None, :] < 4), 2.0 ** 32, 0.0).astype(np.float32),
        "collect": sel,
        "pick0": (np.roll(np.eye(P, 96), 64, 0) * (p >= 64) + np.eye(P, 96, 32) * (p < 64)).astype(np.float32),
        "pick": np.eye(P, 64, dtype=np.float32),
        "k_ones": bf(k_ones),
        "kw_ones": bf(kw_ones),
    }


NAMES = {"L0_attn_x": "x", "L0_attn_Wq": "Wq", "L0_attn_Wk": "Wk", "L0_attn_Wv": "Wv", "L0_attn_Wo": "Wo",
         "L0_attn_Wck": "Wck", "L0_attn_Wcv": "Wcv", "L0_attn_Wg": "Wg", "L0_attn_bg": "bg", "L0_ffn_wg": "wg",
         "L0_ffn_w1": "w1", "L0_ffn_b1": "b1", "L0_ffn_w2": "w2", "L0_ffn_b2": "b2"}


def kernel(**inputs):
    import concourse.bacc as bacc
    import numpy as np
    from concourse.bass_utils import run_bass_kernel_spmd

    nc = bacc.Bacc("TRN2", target_bir_lowering=False, num_devices=1)
    arrays, d = {}, {}
    for name, short in NAMES.items():
        arrays[f"in_{short}"] = np.ascontiguousarray(inputs[name])
        d[short] = arrays[f"in_{short}"]
    for name, a in constants().items():
        arrays[f"const_{name}"] = np.ascontiguousarray(a)
        d[name] = arrays[f"const_{name}"]
    for name, a in list(d.items()):
        prefix = "in_" if f"in_{name}" in arrays else "const_"
        d[name] = nc.dram_tensor(prefix + name, a.shape, mybir.dt.from_np(a.dtype), kind="ExternalInput").ap()
        if a.dtype == np.uint16:
            d[name] = d[name].bitcast(BF16)
    d["out"] = nc.dram_tensor("out_0", (B, T, DM), F32, kind="ExternalOutput").ap()
    d["xn_d"] = nc.dram_tensor("xn_d", (B, T, DM), F32, kind="Internal").ap()
    d["qp_d"] = nc.dram_tensor("qp_d", (3, B * DM, T), BF16, kind="Internal").ap()
    d["kp_d"] = nc.dram_tensor("kp_d", (3, B * DM, TK), BF16, kind="Internal").ap()
    d["tab_d"] = nc.dram_tensor("tab_d", (2 * E * CAP, 1), I32, kind="Internal").ap()
    d["y_d"] = nc.dram_tensor("y_d", (E * CAP, DM), F32, kind="Internal").ap()
    build(nc, d)
    return run_bass_kernel_spmd(nc, [arrays], core_ids=[0]).results[0]["out_0"]
```
